# Optimizing a Trainium2 kernel written in Bass

```python
import numpy as np
import jax
import jax.numpy as jnp

def _softmax(x, axis=-1):
    return jax.nn.softmax(x, axis=axis)

def _gelu(x):
    return jax.nn.gelu(x, approximate=True)

def _silu(x):
    return jax.nn.silu(x)

def _sigmoid(x):
    return jax.nn.sigmoid(x)

def _layernorm(x, axis=-1, eps=1e-05):
    m = jnp.mean(x, axis=axis, keepdims=True)
    v = jnp.var(x, axis=axis, keepdims=True)
    return (x - m) / jnp.sqrt(v + eps)

def _scatter_add(tgt, idx, src, axis=0):
    return tgt.at[idx].add(src)

def _segment_sum(src, seg, n):
    return jax.ops.segment_sum(src, seg, n)
kernel_name = 'mk_gnn_preln_d2_gnn_r32_d4657a'

def setup_inputs(seed: int=0):
    np.random.seed(seed)
    _w = jnp.asarray

    def _rec_inputs():
        import jax
        import jax.numpy as jnp
        _gk = jax.random.key(seed)
        x = -0.0005121 + 1.001 * jax.random.normal(jax.random.fold_in(_gk, 1), (3125, 64), jnp.float32)
        src = jax.random.randint(jax.random.fold_in(_gk, 2), (100000,), 0, 3125, jnp.int32)
        dst = jax.random.randint(jax.random.fold_in(_gk, 3), (100000,), 0, 3125, jnp.int32)
        _o = jnp.argsort(dst, stable=True)
        src = src[_o]
        dst = dst[_o]
        edge_attr_16 = 0.000254156 + 0.999948 * jax.random.normal(jax.random.fold_in(_gk, 11), (100000, 16), jnp.float32)
        return (x, src, dst, edge_attr_16)
    x, src, dst, edge_attr_16 = _rec_inputs()

    def _L0_gnn_setup():
        import jax, jax.numpy as jnp
        import numpy as np
        N, E = (50000, 25000)
        EMB, HEADS, EDGE_DIM = (64, 4, 16)
        NEG_SLOPE = 0.2
        LN_EPS = 1e-05
        key = jax.random.key(seed)
        ks = jax.random.split(key, 12)
        HC = HEADS * EMB
        inp = {'x': jax.random.normal(ks[0], (N, EMB), jnp.float32), 'edge_index': jax.random.randint(ks[1], (2, E), 0, N, jnp.int32), 'edge_attr': jax.random.normal(ks[2], (E, EDGE_DIM), jnp.float32), 'W': jax.random.normal(ks[3], (EMB, HC), jnp.float32) * 0.1, 'W_edge': jax.random.normal(ks[4], (EDGE_DIM, HC), jnp.float32) * 0.1, 'att_src': jax.random.normal(ks[5], (HEADS, EMB), jnp.float32) * 0.1, 'att_dst': jax.random.normal(ks[6], (HEADS, EMB), jnp.float32) * 0.1, 'att_edge': jax.random.normal(ks[7], (HEADS, EMB), jnp.float32) * 0.1, 'bias': jnp.zeros((HC,), jnp.float32), 'Wp': jax.random.normal(ks[8], (HC, EMB), jnp.float32) * 0.05, 'bp': jnp.zeros((EMB,), jnp.float32), 'gamma': jnp.ones((EMB,), jnp.float32), 'beta': jnp.zeros((EMB,), jnp.float32)}
        return inp
    _L0_gnn_all = _L0_gnn_setup()
    _L0_gnn_in = {k: v for k, v in _L0_gnn_all.items() if k in ('W', 'W_edge', 'att_src', 'att_dst', 'att_edge', 'bias', 'Wp', 'bp', 'gamma', 'beta')}
    del _L0_gnn_all

    def _L1_gnn_setup():
        import jax, jax.numpy as jnp
        import numpy as np
        NUM_USERS = 3125
        NUM_MOVIES = 50000
        NUM_NODES = NUM_USERS + NUM_MOVIES
        EMB_DIM = 64
        N_LAYERS = 3
        N_EDGES = 125000
        key = jax.random.key(seed)
        k_e, k_w = jax.random.split(key)
        edge_index = jax.random.randint(k_e, (2, N_EDGES), 0, NUM_NODES, dtype=jnp.int64 if jax.config.jax_enable_x64 else jnp.int32)
        emb_weight = jax.random.normal(k_w, (NUM_NODES, EMB_DIM), dtype=jnp.float32)
        return {'edge_index': edge_index, 'emb_weight': emb_weight}
    _L1_gnn_all = _L1_gnn_setup()
    _L1_gnn_in = {k: v for k, v in _L1_gnn_all.items() if k in ()}
    del _L1_gnn_all
    return {'x': x, 'src': src, 'dst': dst, 'edge_attr_16': edge_attr_16, 'L0_gnn_W': _L0_gnn_in['W'], 'L0_gnn_W_edge': _L0_gnn_in['W_edge'], 'L0_gnn_att_src': _L0_gnn_in['att_src'], 'L0_gnn_att_dst': _L0_gnn_in['att_dst'], 'L0_gnn_att_edge': _L0_gnn_in['att_edge'], 'L0_gnn_bias': _L0_gnn_in['bias'], 'L0_gnn_Wp': _L0_gnn_in['Wp'], 'L0_gnn_bp': _L0_gnn_in['bp'], 'L0_gnn_gamma': _L0_gnn_in['gamma'], 'L0_gnn_beta': _L0_gnn_in['beta']}

def reference(x, src, dst, edge_attr_16, L0_gnn_W, L0_gnn_W_edge, L0_gnn_att_src, L0_gnn_att_dst, L0_gnn_att_edge, L0_gnn_bias, L0_gnn_Wp, L0_gnn_bp, L0_gnn_gamma, L0_gnn_beta):
    import jax
    import jax.numpy as jnp

    def _L0_gnn_ref(x, edge_index, edge_attr, W, W_edge, att_src, att_dst, att_edge, bias, Wp, bp, gamma, beta):
        import jax, jax.numpy as jnp
        import numpy as np
        N, E = (50000, 25000)
        EMB, HEADS, EDGE_DIM = (64, 4, 16)
        NEG_SLOPE = 0.2
        LN_EPS = 1e-05
        n = x.shape[0]
        H, C = att_src.shape
        xw = (x @ W).reshape(n, H, C)
        a_src_n = jnp.einsum('nhc,hc->nh', xw, att_src)
        a_dst_n = jnp.einsum('nhc,hc->nh', xw, att_dst)
        src, dst = (edge_index[0], edge_index[1])
        loop = jnp.arange(n, dtype=edge_index.dtype)
        cnt = jax.ops.segment_sum(jnp.ones_like(dst, jnp.float32), dst, num_segments=n)
        loop_attr = jax.ops.segment_sum(edge_attr, dst, num_segments=n) / jnp.maximum(cnt, 1.0)[:, None]
        src2 = jnp.concatenate([src, loop])
        dst2 = jnp.concatenate([dst, loop])
        ea = jnp.concatenate([edge_attr, loop_attr], axis=0)
        ew = (ea @ W_edge).reshape(-1, H, C)
        a_edge = jnp.einsum('ehc,hc->eh', ew, att_edge)
        alpha = a_src_n[src2] + a_dst_n[dst2] + a_edge
        alpha = jnp.where(alpha >= 0, alpha, NEG_SLOPE * alpha)
        amax = jax.ops.segment_max(alpha, dst2, num_segments=n)
        ae = jnp.exp(alpha - amax[dst2])
        denom = jax.ops.segment_sum(ae, dst2, num_segments=n)
        attn = ae / denom[dst2]
        msg = xw[src2] * attn[:, :, None]
        agg = jax.ops.segment_sum(msg, dst2, num_segments=n)
        gat_out = agg.reshape(n, H * C) + bias
        proj = gat_out @ Wp + bp
        h = x + jax.nn.elu(proj)
        mu = jnp.mean(h, axis=-1, keepdims=True)
        var = jnp.mean((h - mu) ** 2, axis=-1, keepdims=True)
        out = (h - mu) * jax.lax.rsqrt(var + LN_EPS) * gamma + beta
        return out

    def _L1_gnn_ref(edge_index, emb_weight):
        import jax, jax.numpy as jnp
        import numpy as np
        NUM_USERS = 3125
        NUM_MOVIES = 50000
        NUM_NODES = NUM_USERS + NUM_MOVIES
        EMB_DIM = 64
        N_LAYERS = 3
        N_EDGES = 125000
        row, col = (edge_index[0], edge_index[1])
        num_nodes = emb_weight.shape[0]
        deg = jax.ops.segment_sum(jnp.ones_like(col, dtype=emb_weight.dtype), col, num_segments=num_nodes)
        deg_inv_sqrt = jnp.where(deg > 0, jax.lax.rsqrt(jnp.maximum(deg, 1.0)), 0.0)
        deg_inv_sqrt = jnp.where(deg > 0, deg ** (-0.5), 0.0)
        norm = deg_inv_sqrt[row] * deg_inv_sqrt[col]
        embs = emb_weight
        acc = emb_weight
        for _ in range(N_LAYERS):
            msgs = norm[:, None] * embs[row]
            embs = jax.ops.segment_sum(msgs, col, num_segments=num_nodes)
            acc = acc + embs
        return acc / (N_LAYERS + 1)
    edge_index = jnp.stack([src, dst])
    h = jnp.maximum(_layernorm(x, axis=-1), 0.0)
    x = x + _L0_gnn_ref(h, edge_index, edge_attr_16, L0_gnn_W, L0_gnn_W_edge, L0_gnn_att_src, L0_gnn_att_dst, L0_gnn_att_edge, L0_gnn_bias, L0_gnn_Wp, L0_gnn_bp, L0_gnn_gamma, L0_gnn_beta)
    h = jnp.maximum(_layernorm(x, axis=-1), 0.0)
    x = x + _L1_gnn_ref(edge_index, h)
    return x

_drawn_inputs = setup_inputs


def setup_inputs(seed=0):
    import zlib

    import numpy as np

    out = dict(_drawn_inputs(seed))
    spreads = {'L0_gnn_bias': (0.0, 0.1),
     'L0_gnn_bp': (0.0, 0.1),
     'L0_gnn_gamma': (1.0, 0.2),
     'L0_gnn_beta': (0.0, 0.1)}
    factors = {'edge_attr_16': 5.605,
     'L0_gnn_W_edge': 4.332,
     'L0_gnn_att_dst': 200.0,
     'L0_gnn_att_edge': 5.419,
     'L0_gnn_att_src': 4.01}
    for name, (base, spread) in spreads.items():
        noise = np.random.default_rng([zlib.crc32(name.encode()), seed]).standard_normal(out[name].shape)
        drawn = base * np.exp(spread * noise) if base else spread * noise
        out[name] = jnp.asarray(drawn.astype(out[name].dtype))
    for name, factor in factors.items():
        out[name] = (out[name] * factor).astype(out[name].dtype)
    return out
```

```python
from contextlib import ExitStack

import concourse.bass as bass
from concourse import mybir

ALU = mybir.AluOpType
ACT = mybir.ActivationFunctionType
AX = mybir.AxisListType
F32 = mybir.dt.float32
F16 = mybir.dt.float16
BF16 = mybir.dt.bfloat16
I32 = mybir.dt.int32
I16 = mybir.dt.int16

P = 128
N = 3125
D = 64
H = 4
K = 16
E = 100000
Q = 125
NB = N // Q
W = 20
WINDOWS = -(-N // W)
NPAD = WINDOWS * W
EP = 256
PAIRS = 392
STEPS = PAIRS + WINDOWS - 1
WH = W * H
KEYS = W * NB
RING = 4
ROW = D + 1 + H
AGG = D + 1 + K + 1
REC = AGG + 1
BIG = 1e30
CLAMP = -1e20
LRELU = 0.2
EPS = 1e-5
LAYERS = 3
LEAD = 3
assert STEPS % RING == 0 and PAIRS * EP >= E and KEYS <= 512
PARTS = 3


class Chain:

    def __init__(self, eng, sem, per_turn=0):
        self.eng, self.sem, self.per_turn = eng, sem, per_turn
        self.n, self.turn, self.local = 0, None, 0

    def enter_loop(self):
        self.base, self.local = self.n, 0

    def leave_loop(self, turns):
        assert self.local == self.per_turn, self.local
        self.turn = None
        self.n = self.base + turns * self.per_turn

    def did(self, ins):
        ins.then_inc(self.sem, 1)
        if self.turn is None:
            self.n += 1
            return self.n
        self.local += 1
        return (self.turn - 1) * self.per_turn + (self.base + self.local)

    def wait(self, value):
        self.eng.wait_ge(self.sem, value)

    def seq(self, ins):
        self.wait(self.did(ins))


def valid(j):
    return not isinstance(j, int) or 0 <= j < STEPS


def since(eng, sem, j, back, per=1):
    s = j - back
    if isinstance(s, int) and s < 0:
        return
    eng.wait_ge(sem, (s + 1) * per)


def gnn_kernel(nc, x, src_cols, dst_cols, dst_row, last_row, attr_rows, attr_t, w, w_t, w_edge, att_src,
               att_dst, att_edge, bias_t, wp, bp, gamma, beta, out):
    hx_dram = nc.dram_tensor("hx_dram", [N, ROW], F32, kind="Internal").ap()
    ad_dram = nc.dram_tensor("ad_dram", [NPAD, H], F32, kind="Internal").ap()
    m_dram = nc.dram_tensor("m_dram", [1, H * K], F32, kind="Internal").ap()
    rec_dram = nc.dram_tensor("rec_dram", [WINDOWS + STEPS, WH, REC], F32, kind="Internal").ap()

    with ExitStack() as ctx:
        def sem(name):
            return ctx.enter_context(nc.semaphore(name))

        def sb(name, shape, dt, where=ctx):
            return where.enter_context(nc.sbuf_tensor(name, shape, dt))

        psum = [ctx.enter_context(nc.psum_tensor(f"bank{i}", [P, 512], F32)) for i in range(8)]

        counts = sb("counts", [P, NPAD * NB], F16)
        ident = sb("ident", [P, P], F32)
        m_edge = sb("m_edge", [K, H], F32)
        v_out = sb("v_out", [P, 2, D], F32)
        c_out = sb("c_out", [Q, D], F32)

        held = ctx.enter_context(ExitStack())
        plain_sb = sb

        def sb(name, shape, dt, where=held):
            return plain_sb(name, shape, dt, where)

        key = sb("key", [P, 2 * PAIRS], F32)
        dst25 = sb("dst25", [P, 2 * PAIRS], F32)
        src_in = sb("src_in", [P, 2 * PAIRS], F32)
        src_i = sb("src_i", [P, 2 * PAIRS], I32)
        win_dst = sb("win_dst", [P, STEPS], F32)
        win_key = sb("win_key", [P, STEPS], F32)
        restart = sb("restart", [P, STEPS], F32)
        keep = sb("keep", [P, STEPS], F32)
        where_i = sb("where_i", [1, 3, STEPS], I16)

        stage = ctx.enter_context(ExitStack())
        prologue(nc, ctx, stage, psum, sem, sb, locals())
        stage.close()
        stage = ctx.enter_context(ExitStack())
        steps(nc, stage, psum, sem, sb, locals())
        stage.close()
        held.close()
        stage = ctx.enter_context(ExitStack())
        finish(nc, stage, psum, sem, sb, locals())


def prologue(nc, ctx, stage, psum, sem, sb, v):
    ident, m_edge, v_out, c_out = v["ident"], v["m_edge"], v["v_out"], v["c_out"]
    key, dst25, src_in, src_i = v["key"], v["dst25"], v["src_in"], v["src_i"]
    win_dst, win_key, restart, keep, where_i = v["win_dst"], v["win_key"], v["restart"], v["keep"], v["where_i"]
    counts = v["counts"]

    room = [0]

    def tmp(shape, dt, parts=P):
        size = 1
        for s in shape:
            size *= s
        n16 = size * (2 if dt in (F32, I32) else 1)
        ap = counts[0:parts, room[0]:room[0] + n16]
        room[0] += -(-n16 // 16) * 16
        assert room[0] <= NPAD * NB
        ap = ap.bitcast(dt) if dt != F16 else ap
        if len(shape) == 2:
            ap = ap.rearrange("p (a b) -> p a b", a=shape[0])
        elif len(shape) == 3:
            ap = ap.rearrange("p (a b c) -> p a b c", a=shape[0], b=shape[1])
        return ap

    xt = tmp([NB, D], F32, Q)
    sq = tmp([NB, D], F32, Q)
    hx = tmp([NB, ROW], F32, Q)
    a_d = tmp([NB, H], F32, Q)
    h_t = tmp([NB, Q], F32, D)
    stat = tmp([4, NB], F32, Q)
    w_sb = tmp([H * D], F32, D)
    w_ts = tmp([H, D], F32, D)
    wp_s = tmp([H, D], F32, D)
    bias_s = tmp([H], F32, D)
    att_s = tmp([H * D], F32, D)
    att_d = tmp([H * D], F32, D)
    fold = tmp([H * D], F32, D)
    a_sd = tmp([2 * H], F32, D)
    we_s = tmp([H * D], F32, K)
    att_e = tmp([H * D], F32, K)
    fold_e = tmp([H * D], F32, K)
    bp_b = tmp([D], F32, Q)
    last_b = tmp([PAIRS], I32)
    junk = tmp([PAIRS], F32)
    cnt = tmp([2], F32)
    start = tmp([2], F32)
    first = tmp([2], F32)
    edge_at = tmp([2], F32)
    began = tmp([2, STEPS], BF16)
    ones = tmp([P], BF16)
    step_no = tmp([STEPS], F32)
    win = tmp([STEPS], F32)
    same = tmp([STEPS], F32)
    t1 = tmp([STEPS], F32)
    row_i = tmp([2], I32)
    row_w = tmp([2], F32)
    dst_i = tmp([2 * PAIRS], I32)
    s_f = tmp([2 * PAIRS], F32)
    q_i = tmp([2 * PAIRS], I32)
    q_f = tmp([2 * PAIRS], F32)
    adj = tmp([2 * PAIRS], F32)
    zero_h = tmp([H], F32)

    x_in, w_in, e_in, l_in = sem("x_in"), sem("w_in"), sem("e_in"), sem("l_in")
    consts, dchain, gchain = sem("consts"), sem("pro_dve"), sem("pro_pool")
    var_ready, std_ready, h_ready, ht_ready, ht_copied = (
        sem("var_ready"), sem("std_ready"), sem("h_ready"), sem("ht_ready"), sem("ht_copied"))
    sd_ready, a_ready, hx_ready, m_ready, v_ready, v_copied = (
        sem("sd_ready"), sem("pro_a_ready"), sem("hx_ready"), sem("m_ready"), sem("v_ready"), sem("v_copied"))
    began_ready, win_ready, tables_out = sem("began_ready"), sem("win_ready"), sem("tables_out")

    with nc.Block() as block:
        @block.sync
        def _(sp):
            sp.dma_start(xt, v["x"].rearrange("(b p) f -> p b f", p=Q)).then_inc(x_in, 16)
            sp.dma_start(w_sb, v["w"][:, :]).then_inc(w_in, 16)
            sp.dma_start(att_s, v["att_src"].rearrange("h c -> (h c)")[None, :].to_broadcast([D, H * D])).then_inc(w_in, 16)
            sp.dma_start(att_d, v["att_dst"].rearrange("h c -> (h c)")[None, :].to_broadcast([D, H * D])).then_inc(w_in, 16)
            sp.dma_start(we_s, v["w_edge"][:, :]).then_inc(w_in, 16)
            sp.dma_start(att_e, v["att_edge"].rearrange("h c -> (h c)")[None, :].to_broadcast([K, H * D])).then_inc(w_in, 16)
            sp.dma_start(w_ts, v["w_t"].rearrange("(h c) f -> c h f", h=H)).then_inc(w_in, 16)
            sp.dma_start(wp_s, v["wp"].rearrange("(h c) f -> c h f", h=H)).then_inc(w_in, 16)
            sp.dma_start(bias_s, v["bias_t"][:, :]).then_inc(w_in, 16)
            sp.dma_start(bp_b, v["bp"][None, :].to_broadcast([Q, D])).then_inc(w_in, 16)
            sp.dma_start(last_b, v["last_row"][:, :].to_broadcast([P, PAIRS])).then_inc(l_in, 16)
            sp.dma_start(src_i[:, :], v["src_cols"][:, :]).then_inc(e_in, 16)
            sp.dma_start(dst_i, v["dst_cols"][:, :]).then_inc(e_in, 16)
            sp.wait_ge(hx_ready, 1)
            sp.dma_start(v["hx_dram"].rearrange("(b p) f -> p b f", p=Q), hx).then_inc(tables_out, 16)
            sp.dma_start(v["ad_dram"][0:N, :].rearrange("(b p) h -> p b h", p=Q), a_d).then_inc(tables_out, 16)
            sp.wait_ge(consts, 1)
            sp.dma_start(v["ad_dram"][N:NPAD, :], zero_h[0:NPAD - N, :]).then_inc(tables_out, 16)
            sp.wait_ge(m_ready, 1)
            sp.dma_start(v["m_dram"].rearrange("o (h k) -> k h o", h=H), m_edge[:, :].rearrange("k (h o) -> k h o", o=1),
                         allow_slow_non_contiguous=True).then_inc(tables_out, 16)
            sp.wait_ge(tables_out, 64)

        @block.gpsimd
        def _(pool):
            chain = Chain(pool, gchain)
            pool.memset(zero_h, 0.0)
            pool.memset(ones, 1.0)
            pool.memset(hx[:, :, D:D + 1], 1.0)
            chain.seq(pool.memset(ident[:, :], 0.0))
            chain.seq(pool.affine_select(out=ident[:, :], in_=ident[:, :], compare_op=ALU.not_equal, fill=1.0, base=0,
                                         pattern=[[-1, P]], channel_multiplier=1))
            pool.iota(edge_at, pattern=[[P, 2]], base=1, channel_multiplier=1, allow_small_or_imprecise_dtypes=True)
            pool.iota(first, pattern=[[P * W, 2]], base=W, channel_multiplier=W, allow_small_or_imprecise_dtypes=True)
            pool.iota(row_i, pattern=[[0, 2]], base=0, channel_multiplier=1)
            pool.iota(step_no, pattern=[[1, STEPS]], base=0, channel_multiplier=0,
                      allow_small_or_imprecise_dtypes=True).then_inc(consts, 1)

        @block.scalar
        def _(act):
            act.wait_ge(var_ready, 1)
            act.activation(stat[:, 2, :], stat[:, 1, :], ACT.Sqrt).then_inc(std_ready, 1)
            for b in range(NB):
                act.wait_ge(ht_ready, b + 1)
                act.copy(h_t[:, b, :], psum[b % 2][0:D, 0:Q]).then_inc(ht_copied, 1)
            act.wait_ge(v_ready, 1)
            act.copy(v_out[:, :, :], psum[4][:, 0:2 * D].rearrange("p (g f) -> p g f", g=2)).then_inc(v_copied, 1)

        @block.vector
        def _(dve):
            chain = Chain(dve, dchain)
            seq = chain.seq
            dve.wait_ge(l_in, 16)
            dve.wait_ge(consts, 1)
            for g in range(2):
                seq(dve.tensor_scalar(junk, last_b, first[:, g:g + 1], 0.0, ALU.is_lt, ALU.add,
                                      accum_out=cnt[:, g:g + 1]))
            seq(dve.tensor_tensor(out=start, in0=cnt, in1=edge_at, op=ALU.add))
            for g in range(2):
                dve.tensor_scalar(began[:, g, :], step_no, start[:, g:g + 1], None, ALU.is_ge).then_inc(began_ready, 1)
            dve.wait_ge(w_in, 9 * 16)
            for g, a in enumerate((att_s, att_d)):
                seq(dve.tensor_tensor(out=fold, in0=w_sb, in1=a, op=ALU.mult))
                seq(dve.tensor_reduce(a_sd[:, g * H:(g + 1) * H], fold.rearrange("p (h c) -> p h c", h=H), AX.X, ALU.add))
            seq(dve.tensor_tensor(out=fold_e, in0=we_s, in1=att_e, op=ALU.mult))
            dve.tensor_reduce(m_edge[:, :], fold_e.rearrange("p (h c) -> p h c", h=H), AX.X, ALU.add).then_inc(m_ready, 1)
            dve.wait_ge(x_in, 16)
            seq(dve.tensor_reduce(stat[:, 0, :], xt, AX.X, ALU.add))
            seq(dve.tensor_scalar(stat[:, 0, :], stat[:, 0, :], 1.0 / D, None, ALU.mult))
            seq(dve.tensor_tensor(out=xt, in0=xt, in1=stat[:, 0, :].unsqueeze(2).to_broadcast([Q, NB, D]), op=ALU.subtract))
            seq(dve.tensor_tensor(out=sq, in0=xt, in1=xt, op=ALU.mult))
            seq(dve.tensor_reduce(stat[:, 1, :], sq, AX.X, ALU.add))
            dve.tensor_scalar(stat[:, 1, :], stat[:, 1, :], 1.0 / D, EPS, ALU.mult, ALU.add).then_inc(var_ready, 1)
            dve.wait_ge(std_ready, 1)
            seq(dve.reciprocal(stat[:, 3, :], stat[:, 2, :]))
            seq(dve.tensor_tensor(out=xt, in0=xt, in1=stat[:, 3, :].unsqueeze(2).to_broadcast([Q, NB, D]), op=ALU.mult))
            dve.tensor_scalar(hx[:, :, 0:D], xt, 0.0, None, ALU.max).then_inc(h_ready, 1)
            dve.wait_ge(e_in, 32)
            seq(dve.tensor_copy(s_f, src_i[:, :]))
            seq(dve.tensor_scalar(q_i, s_f, 1.0 / Q, None, ALU.mult))
            seq(dve.tensor_copy(q_f, q_i))
            seq(dve.scalar_tensor_tensor(src_in[:, :], q_f, -float(Q), s_f, ALU.mult, ALU.add))
            for bound, op, sign in ((0.0, ALU.is_lt, 1.0), (float(Q), ALU.is_ge, -1.0)):
                seq(dve.tensor_scalar(adj, src_in[:, :], bound, sign, op, ALU.mult))
                seq(dve.scalar_tensor_tensor(src_in[:, :], adj, float(Q), src_in[:, :], ALU.mult, ALU.add))
                seq(dve.tensor_tensor(out=q_f, in0=q_f, in1=adj, op=ALU.subtract))
            seq(dve.tensor_scalar(dst25[:, :], dst_i, float(NB), None, ALU.mult))
            seq(dve.tensor_tensor(out=key[:, :], in0=dst25[:, :], in1=q_f, op=ALU.add))
            half = STEPS // 2
            dve.wait_ge(win_ready, 1)
            for g in range(2):
                seq(dve.tensor_copy(win[:, g * half:(g + 1) * half], psum[2 + g][:, 0:half]))
            seq(dve.tensor_scalar(win_key[:, :], win, float(KEYS), None, ALU.mult))
            seq(dve.tensor_scalar(row_i, row_i, 2, None, ALU.arith_shift_right))
            seq(dve.tensor_copy(row_w, row_i))
            seq(dve.tensor_scalar(win_dst[:, :], win, float(W), row_w[:, 0:1], ALU.mult, ALU.add))
            seq(dve.memset(keep[:, 0:1], 0.0))
            seq(dve.tensor_tensor(out=keep[:, 1:STEPS], in0=win[:, 1:STEPS], in1=win[:, 0:STEPS - 1], op=ALU.is_equal))
            seq(dve.tensor_scalar(restart[:, :], keep[:, :], 1.0, BIG, ALU.subtract, ALU.mult))
            seq(dve.tensor_tensor(out=t1, in0=step_no, in1=win, op=ALU.subtract))
            seq(dve.tensor_copy(where_i[0:1, 0, :], t1[0:1, :]))
            seq(dve.tensor_copy(where_i[0:1, 1, :], win[0:1, :]))
            seq(dve.memset(same[:, STEPS - 1:STEPS], 0.0))
            seq(dve.tensor_copy(same[:, 0:STEPS - 1], keep[:, 1:STEPS]))
            seq(dve.scalar_tensor_tensor(t1, t1, float(WINDOWS), same, ALU.add, ALU.mult))
            seq(dve.tensor_tensor(out=where_i[0:1, 2, :], in0=t1[0:1, :], in1=win[0:1, :], op=ALU.add))
            dve.wait_ge(a_ready, 1)
            pa = psum[5][0:Q, 0:NB * 2 * H].rearrange("p (b g) -> p b g", b=NB)
            seq(dve.tensor_copy(hx[:, :, D + 1:ROW], pa[:, :, 0:H]))
            dve.tensor_copy(a_d, pa[:, :, H:2 * H]).then_inc(hx_ready, 1)
            dve.wait_ge(v_ready, 2)
            seq(dve.tensor_tensor(out=c_out[:, :], in0=psum[6][0:Q, 0:D], in1=bp_b, op=ALU.add))

        @block.tensor
        def _(pe):
            pe.wait_ge(consts, 1)
            pe.wait_ge(began_ready, 2)
            half = STEPS // 2
            for g in range(2):
                for s in range(2):
                    last = pe.matmul(psum[2 + g][:, 0:half], ones, began[:, s, g * half:(g + 1) * half],
                                     start=s == 0, stop=s == 1)
            last.then_inc(win_ready, 1)
            pe.wait_ge(w_in, 9 * 16)
            for h in range(H):
                o = D * (h % 2)
                last = pe.matmul(psum[4][o:o + D, D * (h // 2):D * (h // 2) + D], w_ts[:, h, :], wp_s[:, h, :],
                                 start=True, stop=True)
            last.then_inc(v_ready, 1)
            for h in range(H):
                last = pe.matmul(psum[6][0:Q, 0:D], bias_s[:, h:h + 1].to_broadcast([D, Q]), wp_s[:, h, :],
                                 start=h == 0, stop=h == H - 1)
            last.then_inc(v_ready, 1)
            pe.wait_ge(h_ready, 1)
            for b in range(NB):
                if b >= 2:
                    pe.wait_ge(ht_copied, b - 1)
                pe.transpose(psum[b % 2][0:D, 0:Q], hx[:, b, 0:D], ident[0:Q, 0:Q]).then_inc(ht_ready, 1)
            pe.wait_ge(ht_copied, NB)
            pe.wait_ge(m_ready, 1)
            for b in range(NB):
                last = pe.matmul(psum[5][0:Q, b * 2 * H:(b + 1) * 2 * H], h_t[:, b, :], a_sd, start=True, stop=True)
            last.then_inc(a_ready, 1)


def steps(nc, stage, psum, sem, sb, v):
    ident, m_edge = v["ident"], v["m_edge"]
    key, dst25, src_in, src_i = v["key"], v["dst25"], v["src_in"], v["src_i"]
    win_dst, win_key, restart, keep, where_i = v["win_dst"], v["win_key"], v["restart"], v["keep"], v["where_i"]
    counts = v["counts"]

    def t(name, shape, dt):
        return sb(name, shape, dt, stage)

    idx = t("idx", [P, RING, 2], I32)
    rows = t("rows", [P, RING, 2, ROW], F32)
    attr_e = t("attr_e", [P, RING, 2, K + 1], F32)
    AT = 96
    along = t("along", [AT + K + 1, RING, EP], F32)
    dst_b = along[0:WH, :, :].bitcast(I32)
    attr_w = along[AT:AT + K + 1, :, :]
    off = t("off", [WH, EP], F32)
    logit = t("logit", [WH, 2, EP], F32)
    prob = t("prob", [WH, 2, EP], F32)
    weight = t("weight", [P, 2, 2, WH], F32)
    rel = t("rel", [P, 2, 4], F32)
    hot_key = t("hot_key", [P, 2, 2, KEYS], F16)
    hot_src = t("hot_src", [P, 2, 2, Q], F16)
    hot_dst = t("hot_dst", [P, RING, 2, WH], F32)
    src_wh = t("src_wh", [P, 2, 2, WH], F32)
    m_wh = t("m_wh_all", [AT + K + 1, RING, WH], F32)[AT:AT + K + 1, :, :]
    rec = t("rec", [WH, RING, REC], F32)
    top = t("top", [WH, RING], F32)
    top_new = t("top_new", [WH, RING], F32)
    carry = t("carry", [WH, RING], F32)
    m = t("m", [WH, RING], F32)
    m_neg = t("m_neg", [WH, RING], F32)
    m_diff = t("m_diff", [WH, RING], F32)
    scale = t("scale", [WH, RING], F32)
    num_key = t("num_key", [P, KEYS], F16)
    num_src = t("num_src", [P, Q], F16)
    num_dst = t("num_dst", [P, WH], F32)
    none = t("none", [P, 1], I32)
    none2 = t("none2", [P, 1], I32)

    dchain, opened = sem("step_dve"), sem("opened")
    ready0 = sem("step_consts")
    staged = sem("indices_staged")
    gathered = [sem(f"gathered{k}") for k in range(RING)]
    loaded = [sem(f"loaded{k}") for k in range(RING)]
    stored = [sem(f"stored{k}") for k in range(RING)]
    hot_ready, adj_ready, adj_added = sem("hot_ready"), sem("adj_ready"), sem("adj_added")
    u_ready, logit_ready, prob_ready = sem("u_ready"), sem("logit_ready"), sem("prob_ready")
    turned, weight_ready = sem("turned"), sem("weight_ready")
    agg_ready, rec_ready = sem("agg_ready"), sem("rec_ready")
    spread, m_spread = sem("spread"), sem("m_spread")

    ps_u = [psum[0], psum[1]]
    ps_w = [psum[2], psum[3]]
    ps_g = [psum[4], psum[5]]
    ps_a = [psum[6], psum[7]]

    CONSTS = 6
    with nc.Block() as block:
        def walk(eng, body, chain=None):
            for j in range(-RING, RING):
                body(j, j, None)
            turns = STEPS // RING
            if chain is not None:
                chain.enter_loop()
            with eng.Fori(1, turns - 1) as n:
                if chain is not None:
                    chain.turn = n
                for k in range(RING):
                    body(n * RING + k, k, n)
            if chain is not None:
                chain.leave_loop(turns - 2)
            for j in range((turns - 1) * RING, STEPS + RING):
                body(j, j, None)

        def slot_count(k, d, n, per):
            s = k + d
            return (s // RING + 1) * per if n is None else (n + (s // RING + 1)) * per

        @block.sync
        def _(sp):
            sp.wait_ge(ready0, CONSTS)

            def body(j, k, n):
                s = j - LEAD
                if valid(s):
                    sp.wait_ge(rec_ready, s + 1)
                    r = sp.value_load(where_i[0:1, 2, bass.ds(s, 1)], min_val=0, max_val=WINDOWS + STEPS - 1)
                    sp.dma_start(v["rec_dram"][bass.ds(r, 1), :, :].rearrange("o q f -> (o q) f"),
                                 rec[:, (k - LEAD) % RING, :]).then_inc(stored[(k - LEAD) % RING], 16)
                s = j + LEAD
                if valid(s):
                    c = (k + LEAD) % RING
                    since(sp, agg_ready, s, RING)
                    r = sp.value_load(where_i[0:1, 0, bass.ds(s, 1)], min_val=0, max_val=PAIRS - 1)
                    b = sp.value_load(where_i[0:1, 1, bass.ds(s, 1)], min_val=0, max_val=WINDOWS - 1)
                    sp.dma_start(m_wh[K:K + 1, c, :], v["ad_dram"][bass.ds(b * W, W), :].rearrange("(o w) h -> o (w h)", o=1)).then_inc(loaded[c], 16)
                    sp.dma_start(attr_w[0:K, c, :], v["attr_t"][:, bass.ds(r * EP, EP)]).then_inc(loaded[c], 16)
                    sp.dma_start(dst_b[:, c, :], v["dst_row"][:, bass.ds(r * EP, EP)].to_broadcast([WH, EP])).then_inc(loaded[c], 16)
                    sp.dma_start(attr_e[:, c, :, 0:K],
                                 v["attr_rows"][bass.ds(r, 1), :, :, :].rearrange("o p a f -> (o p) a f")).then_inc(loaded[c], 16)
            walk(sp, body)
            for k in range(RING):
                sp.wait_ge(stored[k], STEPS // RING * 16)

        @block.gpsimd
        def _(pool):
            chain = Chain(pool, ready0)
            chain.seq(pool.iota(num_key[:, :], pattern=[[1, KEYS]], base=0, channel_multiplier=0, allow_small_or_imprecise_dtypes=True))
            chain.seq(pool.iota(num_src[:, :], pattern=[[1, Q]], base=0, channel_multiplier=0, allow_small_or_imprecise_dtypes=True))
            chain.seq(pool.iota(num_dst[:, :], pattern=[[NB, W], [0, H]], base=0, channel_multiplier=0, allow_small_or_imprecise_dtypes=True))
            chain.seq(pool.memset(attr_e[:, :, :, K:K + 1], 1.0))
            chain.seq(pool.memset(attr_w, 1.0))
            chain.seq(pool.memset(none[:, :], 0))

            def body(j, k, n):
                s = j + LEAD
                if not valid(s):
                    return
                c = (k + LEAD) % RING
                since(pool, agg_ready, s, RING)
                pool.wait_ge(staged, s + 1)
                since(pool, opened, s, 1)
                pool.tensor_tensor(out=none2[:, :], in0=none[:, :], in1=none[:, :], op=ALU.add).then_inc(opened, 1)
                for a in range(2):
                    pool.indirect_dma_start(rows[:, c, a, :], None, v["hx_dram"][:, :],
                                            bass.IndirectOffsetOnAxis(ap=idx[:, c, a:a + 1], axis=0)).then_inc(gathered[c], 16)
            walk(pool, body)

        @block.scalar
        def _(act):

            for c in range(RING):
                act.copy(m_wh[0:K, c, :].rearrange("k (w h) -> k w h", w=W),
                         m_edge[:, None, :].to_broadcast([K, W, H])).then_inc(m_spread, 1)

            def body(j, k, n):
                s = j + LEAD + 1
                if valid(s):
                    c = (k + LEAD + 1) % RING
                    if not isinstance(s, int) or s >= RING:
                        act.wait_ge(gathered[c], slot_count(k, LEAD + 1 - RING, n, 32))
                    r = act.value_load(where_i[0:1, 0, bass.ds(s, 1)], min_val=0, max_val=PAIRS - 1)
                    act.copy(idx[:, c, :], src_i[:, bass.ds(r * 2, 2)]).then_inc(staged, 1)
                s = j + 1
                if valid(s):
                    c = (k + 1) % RING
                    act.wait_ge(gathered[c], slot_count(k, 1, n, 32))
                    since(act, u_ready, s, 2)
                    act.copy(src_wh[:, c % 2, :, :].rearrange("p a (w h) -> p a w h", w=W),
                             rows[:, c, :, None, D + 1:ROW].to_broadcast([P, 2, W, H])).then_inc(spread, 1)
                s = j
                if valid(s):
                    c = k % RING
                    act.wait_ge(logit_ready, s + 1)
                    since(act, turned, s, 2)
                    act.activation(scale[:, c:c + 1], m_diff[:, c:c + 1], ACT.Exp)
                    act.activation(prob[:, c % 2, :], logit[:, c % 2, :], ACT.Exp, bias=m_neg[:, c:c + 1]).then_inc(prob_ready, 1)
                s = j - 1
                if valid(s):
                    c = (k - 1) % RING
                    act.wait_ge(turned, s + 1)
                    since(act, agg_ready, s, 2)
                    act.copy(weight[:, c % 2, :, :], ps_w[c % 2][:, 0:2 * WH].rearrange("p (a q) -> p a q", a=2)).then_inc(weight_ready, 1)
            walk(act, body)

        @block.vector
        def _(dve):
            chain = Chain(dve, dchain, per_turn=13 * RING)
            did = chain.did
            chain.seq(dve.memset(counts[:, :], 0.0))
            did(dve.memset(rec[:, :, :], 0.0))
            did(dve.memset(top_new[:, :], 0.0))
            chain.seq(dve.memset(m[:, :], 0.0))
            dve.wait_ge(ready0, CONSTS)

            def body(j, k, n):
                s = j + 1
                if valid(s):
                    c = (k + 1) % RING
                    g = c % 2
                    r = dve.value_load(where_i[0:1, 0, bass.ds(s, 1)], min_val=0, max_val=PAIRS - 1)
                    a0 = did(dve.tensor_scalar(rel[:, g, 0:2], key[:, bass.ds(r * 2, 2)], win_key[:, bass.ds(s, 1)], None, ALU.subtract))
                    a1 = did(dve.tensor_scalar(rel[:, g, 2:4], dst25[:, bass.ds(r * 2, 2)], win_key[:, bass.ds(s, 1)], None, ALU.subtract))
                    since(dve, adj_ready, s, 2)
                    since(dve, agg_ready, s, RING)
                    for a in range(2):
                        did(dve.tensor_scalar(hot_src[:, g, a, :], num_src[:, :], src_in[:, bass.ds(r * 2 + a, 1)], None, ALU.is_equal))
                    chain.wait(a1)
                    did(dve.tensor_tensor(out=hot_dst[:, c, :, :], in0=num_dst[:, None, :].to_broadcast([P, 2, WH]),
                                          in1=rel[:, g, 2:4].unsqueeze(2).to_broadcast([P, 2, WH]), op=ALU.is_equal))
                    did(dve.tensor_scalar(hot_key[:, g, 0, :], num_key[:, :], rel[:, g, 0:1], 0.5, ALU.is_equal, ALU.mult))
                    dve.tensor_scalar(hot_key[:, g, 1, :], num_key[:, :], rel[:, g, 1:2], 0.5, ALU.is_equal, ALU.mult).then_inc(hot_ready, 1)
                s = j
                if valid(s):
                    c = k % RING
                    b = dve.value_load(where_i[0:1, 1, bass.ds(s, 1)], min_val=0, max_val=WINDOWS - 1)
                    dve.wait_ge(loaded[c], slot_count(k, 0, n, 64))
                    off_done = did(dve.tensor_scalar(off[:, :], dst_b[:, c, :], win_dst[0:WH, bass.ds(s, 1)], -BIG,
                                                     ALU.not_equal, ALU.mult))
                    dve.wait_ge(u_ready, s + 1)
                    since(dve, prob_ready, s, 2)
                    chain.wait(off_done)
                    did(dve.tensor_copy(carry[:, c:c + 1], restart[0:WH, bass.ds(s, 1)]))
                    u_done = did(dve.tensor_tensor_reduce(out=logit[:, c % 2, :], in0=ps_u[c % 2][0:WH, 0:EP], in1=off[:, :],
                                                          scale=1.0, scalar=CLAMP, op0=ALU.add, op1=ALU.max,
                                                          accum_out=top[:, c:c + 1]))
                    dve.wait_ge(adj_ready, s + 1)
                    here = counts[0:Q, bass.ds(b * KEYS, KEYS)]
                    dve.tensor_tensor(out=here, in0=ps_a[c % 2][0:Q, 0:KEYS], in1=here, op=ALU.add).then_inc(adj_added, 1)
                    prev = (c - 1) % RING
                    chain.wait(u_done)
                    z = did(dve.scalar_tensor_tensor(top_new[:, c:c + 1], top_new[:, prev:prev + 1], restart[0:WH, bass.ds(s, 1)],
                                                     top[:, c:c + 1], ALU.add, ALU.max))
                    did(dve.scalar_tensor_tensor(logit[:, c % 2, :], logit[:, c % 2, :], LRELU, logit[:, c % 2, :], ALU.mult, ALU.max))
                    chain.wait(z)
                    z = did(dve.scalar_tensor_tensor(m[:, c:c + 1], top_new[:, c:c + 1], LRELU, top_new[:, c:c + 1], ALU.mult, ALU.max))
                    chain.wait(z)
                    did(dve.scalar_tensor_tensor(m_diff[:, c:c + 1], m[:, prev:prev + 1], restart[0:WH, bass.ds(s, 1)],
                                                 m[:, c:c + 1], ALU.add, ALU.subtract))
                    dve.tensor_scalar(m_neg[:, c:c + 1], m[:, c:c + 1], -1.0, None, ALU.mult).then_inc(logit_ready, 1)
                s = j - 2
                if valid(s):
                    c = (k - 2) % RING
                    prev = (c - 1) % RING
                    dve.wait_ge(agg_ready, s + 1)
                    if not isinstance(s, int) or s >= RING:
                        dve.wait_ge(stored[c], slot_count(k, -2 - RING, n, 16))
                    since(dve, rec_ready, s, 1)
                    dve.scalar_tensor_tensor(rec[:, c, 0:D + 1], rec[:, prev, 0:D + 1], scale[:, c:c + 1],
                                             ps_g[c % 2][0:WH, 0:D + 1], ALU.mult, ALU.add)
                    dve.tensor_copy(rec[:, c, AGG:REC], m[:, c:c + 1])
                    dve.scalar_tensor_tensor(rec[:, c, D + 1:AGG], rec[:, prev, D + 1:AGG], keep[0:WH, bass.ds(s, 1)],
                                             ps_g[c % 2][0:WH, D + 1:AGG], ALU.mult, ALU.add).then_inc(rec_ready, 1)
            walk(dve, body, chain)

        @block.tensor
        def _(pe):
            pe.wait_ge(ready0, CONSTS)
            pe.wait_ge(m_spread, RING)

            def body(j, k, n):
                s = j
                if valid(s):
                    c = k % RING
                    pe.wait_ge(loaded[c], slot_count(k, 0, n, 64))
                    pe.wait_ge(spread, s + 1)
                    since(pe, logit_ready, s, 2)
                    pe.matmul(ps_u[c % 2][0:WH, 0:EP], m_wh[:, c, :], attr_w[:, c, :],
                              start=True, stop=False)
                    for a in range(2):
                        last = pe.matmul(ps_u[c % 2][0:WH, a * P:(a + 1) * P],
                                         src_wh[:, c % 2, a, :], ident[:, :],
                                         start=False, stop=a == 1)
                    last.then_inc(u_ready, 1)
                    pe.wait_ge(hot_ready, s + 1)
                    since(pe, adj_added, s, 2)
                    for a in range(2):
                        last = pe.matmul(ps_a[c % 2][0:Q, 0:KEYS], hot_src[:, c % 2, a, :], hot_key[:, c % 2, a, :],
                                         start=a == 0, stop=a == 1)
                    last.then_inc(adj_ready, 1)
                s = j - 1
                if valid(s):
                    c = (k - 1) % RING
                    pe.wait_ge(prob_ready, s + 1)
                    since(pe, weight_ready, s, 2)
                    for a in range(2):
                        last = pe.transpose(ps_w[c % 2][:, a * WH:(a + 1) * WH], prob[:, c % 2, a * P:(a + 1) * P],
                                            ident[0:WH, 0:WH])
                    last.then_inc(turned, 1)
                s = j - 2
                if valid(s):
                    c = (k - 2) % RING
                    pe.wait_ge(weight_ready, s + 1)
                    since(pe, rec_ready, s, 2)
                    for a in range(2):
                        pe.matmul(ps_g[c % 2][0:WH, 0:D + 1], weight[:, c % 2, a, :], rows[:, c, a, 0:D + 1],
                                  start=a == 0, stop=a == 1)
                    for a in range(2):
                        last = pe.matmul(ps_g[c % 2][0:WH, D + 1:AGG],
                                         hot_dst[:, c, a, :], attr_e[:, c, a, :],
                                         start=a == 0, stop=a == 1)
                    last.then_inc(agg_ready, 1)
            walk(pe, body)


def finish(nc, stage, psum, sem, sb, v):
    ident, counts, v_out, c_out = v["ident"], v["counts"], v["v_out"], v["c_out"]

    def t(name, shape, dt):
        return sb(name, shape, dt, stage)

    CH = 5
    agg = t("agg", [Q, 2, CH, H, REC], F32)
    hx = t("hx", [Q, NB, ROW], F32)
    a_d = t("a_d", [Q, NB, H], F32)
    m_b = t("m_b", [Q, H, K], F32)
    x_s = t("x_s", [Q, NB, D], F32)
    g_b = t("g_b", [Q, 2, D], F32)
    small = t("small", [Q, 8, CH, H], F32)
    deg = t("deg", [Q, NB], F32)
    cmax = t("cmax", [Q, 2, CH], F32)
    mix = t("mix", [Q, 2, CH, H, D], F32)
    turned_s = t("turned_s", [P, 4, Q], F32)
    cur = t("cur", [Q, NB, D], F32)
    work = t("work", [Q, NB, D], F32)
    stat = t("stat", [Q, 4, NB], F32)
    dinv = t("dinv", [Q, 2, NB], F32)
    mix2 = work[:, :, :].rearrange("p b f -> p (b f)")[:, 0:CH * H * D].rearrange("p (b h f) -> p b h f", b=CH, h=H)
    attr_m = work[:, :, :].rearrange("p b f -> p (b f)")[:, CH * H * D:CH * (H * D + K)].rearrange("p (b k) -> p b k", b=CH)
    parts = mix[:, :, :, :, :].rearrange("p a b h f -> p (a b h f)").bitcast(BF16)[:, 0:NB * PARTS * D].rearrange(
        "p (b s f) -> p b s f", b=NB, s=PARTS)

    in_s, rec_in = sem("fin_in"), [sem("rec_in0"), sem("rec_in1")]
    dchain = sem("fin_dve")
    diff, exps = sem("fin_diff"), sem("fin_exps")
    mix_ready, tr_ready, tr_copied, proj_ready, proj_taken = (
        sem("mix_ready"), sem("tr_ready"), sem("tr_copied"), sem("proj_ready"), sem("proj_taken"))
    act_ask, act_done = sem("act_ask"), sem("act_done")
    parts_ready, prop_ready, prop_taken = sem("parts_ready"), sem("prop_ready"), sem("prop_taken")
    out_ready, out_done = sem("out_ready"), sem("out_done")
    chunks = NB // CH

    def bc(ap, shape):
        return ap.unsqueeze(len(shape) - 1).to_broadcast(shape)

    with nc.Block() as block:
        @block.sync
        def _(sp):
            sp.dma_start(hx[:, :, :], v["hx_dram"].rearrange("(b p) f -> p b f", p=Q)).then_inc(in_s, 16)
            sp.dma_start(a_d[:, :, :], v["ad_dram"][0:N, :].rearrange("(b p) h -> p b h", p=Q)).then_inc(in_s, 16)
            sp.dma_start(m_b[:, :, :], v["m_dram"].rearrange("o (h k) -> o h k", h=H).to_broadcast([Q, H, K])).then_inc(in_s, 16)
            sp.dma_start(x_s[:, :, :], v["x"].rearrange("(b p) f -> p b f", p=Q)).then_inc(in_s, 16)
            sp.dma_start(g_b[:, 0, :], v["gamma"][None, :].to_broadcast([Q, D])).then_inc(in_s, 16)
            sp.dma_start(g_b[:, 1, :], v["beta"][None, :].to_broadcast([Q, D])).then_inc(in_s, 16)
            nodes = v["rec_dram"][0:WINDOWS, :, :].rearrange("b (w h) f -> (b w) (h f)", w=W)
            for c in range(chunks):
                if c >= 2:
                    sp.wait_ge(mix_ready, c - 1)
                part = nodes[c * CH * Q:(c + 1) * CH * Q, :].rearrange("(b p) f -> p b f", p=Q)
                sp.dma_start(agg[:, c % 2, :, :, :].rearrange("p b h f -> p b (h f)"), part).then_inc(rec_in[c % 2], 16)
            sp.wait_ge(out_ready, 1)
            sp.dma_start(v["out"].rearrange("(b p) f -> p b f", p=Q), work[:, :, :]).then_inc(out_done, 16)
            sp.wait_ge(out_done, 16)

        @block.scalar
        def _(act):
            for c in range(chunks):
                act.wait_ge(diff, c + 1)
                act.activation(small[:, 4:6, :, :], small[:, 2:4, :, :], ACT.Exp).then_inc(exps, 1)
                for b in range(CH):
                    for g in range(2):
                        i = (c * CH + b) * 2 + g
                        act.wait_ge(tr_ready, i + 1)
                        if i >= 4:
                            act.wait_ge(proj_ready, (i - 4) // 2 + 1)
                        act.copy(turned_s[:, i % 4, :], psum[i % 2][:, 0:Q]).then_inc(tr_copied, 1)
            act.wait_ge(act_ask, 1)
            act.activation(work[:, :, :], work[:, :, :], ACT.Exp).then_inc(act_done, 1)
            for i in range(2):
                act.wait_ge(act_ask, i + 2)
                act.activation(stat[:, 2, :], stat[:, 1, :], ACT.Sqrt).then_inc(act_done, 1)
            act.wait_ge(act_ask, 4)
            act.activation(dinv[:, 1, :], deg[:, :], ACT.Sqrt).then_inc(act_done, 1)

        @block.vector
        def _(dve):
            chain = Chain(dve, dchain)
            seq = chain.seq
            dve.wait_ge(in_s, 6 * 16)
            for c in range(chunks):
                blocks = slice(c * CH, (c + 1) * CH)
                a = agg[:, c % 2, :, :, :]
                dve.wait_ge(rec_in[c % 2], (c // 2 + 1) * 16)
                cnt = a[:, :, 0, AGG - 1]
                seq(dve.tensor_copy(deg[:, blocks], cnt))
                seq(dve.tensor_scalar(cmax[:, 0, :], cnt, 1.0, None, ALU.max))
                seq(dve.reciprocal(cmax[:, 1, :], cmax[:, 0, :]))
                for h in range(H):
                    seq(dve.tensor_tensor(out=attr_m[:, :, :], in0=a[:, :, 0, D + 1:D + 1 + K],
                                          in1=m_b[:, h, None, :].to_broadcast([Q, CH, K]), op=ALU.mult))
                    seq(dve.tensor_reduce(small[:, 0, :, h], attr_m[:, :, :], AX.X, ALU.add))
                seq(dve.tensor_tensor(out=small[:, 0, :, :], in0=small[:, 0, :, :], in1=bc(cmax[:, 1, :], [Q, CH, H]), op=ALU.mult))
                seq(dve.tensor_tensor(out=small[:, 0, :, :], in0=small[:, 0, :, :], in1=hx[:, blocks, D + 1:ROW], op=ALU.add))
                seq(dve.tensor_tensor(out=small[:, 0, :, :], in0=small[:, 0, :, :], in1=a_d[:, blocks, :], op=ALU.add))
                seq(dve.scalar_tensor_tensor(small[:, 1, :, :], small[:, 0, :, :], LRELU, small[:, 0, :, :], ALU.mult, ALU.max))
                m_e = a[:, :, :, AGG]
                seq(dve.tensor_tensor(out=small[:, 0, :, :], in0=small[:, 1, :, :], in1=m_e, op=ALU.max))
                seq(dve.tensor_tensor(out=small[:, 2, :, :], in0=m_e, in1=small[:, 0, :, :], op=ALU.subtract))
                dve.tensor_tensor(out=small[:, 3, :, :], in0=small[:, 1, :, :], in1=small[:, 0, :, :], op=ALU.subtract).then_inc(diff, 1)
                dve.wait_ge(exps, c + 1)
                seq(dve.tensor_tensor(out=small[:, 6, :, :], in0=small[:, 4, :, :], in1=a[:, :, :, D], op=ALU.mult))
                seq(dve.tensor_tensor(out=small[:, 6, :, :], in0=small[:, 6, :, :], in1=small[:, 5, :, :], op=ALU.add))
                seq(dve.reciprocal(small[:, 7, :, :], small[:, 6, :, :]))
                for g in (4, 5):
                    seq(dve.tensor_tensor(out=small[:, g, :, :], in0=small[:, g, :, :], in1=small[:, 7, :, :], op=ALU.mult))
                if c >= 2:
                    dve.wait_ge(tr_ready, (c - 1) * CH * 2)
                mx = mix[:, c % 2, :, :, :]
                for h in range(H):
                    did = chain.did(dve.tensor_tensor(out=mx[:, :, h, :], in0=a[:, :, h, 0:D], in1=bc(small[:, 4, :, h], [Q, CH, D]), op=ALU.mult))
                    did = chain.did(dve.tensor_tensor(out=mix2[:, :, h, :], in0=hx[:, blocks, 0:D], in1=bc(small[:, 5, :, h], [Q, CH, D]), op=ALU.mult))
                chain.wait(did)
                dve.tensor_tensor(out=mx, in0=mx, in1=mix2[:, :, :, :], op=ALU.add).then_inc(mix_ready, 1)
                dve.wait_ge(mix_ready, c + 1)
                dve.wait_ge(proj_ready, (c + 1) * CH)
                pr = psum[2 + c % 2][0:Q, 0:CH * D].rearrange("p (b f) -> p b f", b=CH)
                dve.tensor_tensor(out=cur[:, blocks, :], in0=pr, in1=c_out[:, None, :].to_broadcast([Q, CH, D]), op=ALU.add).then_inc(proj_taken, 1)
            dve.wait_ge(proj_taken, chunks)
            dve.tensor_scalar(work[:, :, :], cur[:, :, :], 0.0, None, ALU.min).then_inc(act_ask, 1)
            dve.wait_ge(act_done, 1)
            seq(dve.tensor_scalar(cur[:, :, :], cur[:, :, :], 0.0, None, ALU.max))
            seq(dve.scalar_tensor_tensor(cur[:, :, :], work[:, :, :], -1.0, cur[:, :, :], ALU.add, ALU.add))
            seq(dve.tensor_tensor(out=cur[:, :, :], in0=cur[:, :, :], in1=hx[:, :, 0:D], op=ALU.add))

            def norm(i):
                seq(dve.tensor_reduce(stat[:, 0, :], cur[:, :, :], AX.X, ALU.add))
                seq(dve.tensor_scalar(stat[:, 0, :], stat[:, 0, :], 1.0 / D, None, ALU.mult))
                seq(dve.tensor_tensor(out=cur[:, :, :], in0=cur[:, :, :], in1=bc(stat[:, 0, :], [Q, NB, D]), op=ALU.subtract))
                seq(dve.tensor_tensor(out=work[:, :, :], in0=cur[:, :, :], in1=cur[:, :, :], op=ALU.mult))
                seq(dve.tensor_reduce(stat[:, 1, :], work[:, :, :], AX.X, ALU.add))
                dve.tensor_scalar(stat[:, 1, :], stat[:, 1, :], 1.0 / D, EPS, ALU.mult, ALU.add).then_inc(act_ask, 1)
                dve.wait_ge(act_done, i + 2)
                seq(dve.reciprocal(stat[:, 3, :], stat[:, 2, :]))
                seq(dve.tensor_tensor(out=cur[:, :, :], in0=cur[:, :, :], in1=bc(stat[:, 3, :], [Q, NB, D]), op=ALU.mult))

            norm(0)
            seq(dve.tensor_tensor(out=cur[:, :, :], in0=cur[:, :, :], in1=g_b[:, 0, None, :].to_broadcast([Q, NB, D]), op=ALU.mult))
            seq(dve.tensor_tensor(out=cur[:, :, :], in0=cur[:, :, :], in1=g_b[:, 1, None, :].to_broadcast([Q, NB, D]), op=ALU.add))
            seq(dve.tensor_tensor(out=x_s[:, :, :], in0=x_s[:, :, :], in1=cur[:, :, :], op=ALU.add))
            seq(dve.tensor_copy(cur[:, :, :], x_s[:, :, :]))
            norm(1)
            seq(dve.tensor_scalar(cur[:, :, :], cur[:, :, :], 0.0, None, ALU.max))
            seq(dve.scalar_tensor_tensor(x_s[:, :, :], cur[:, :, :], 1.0 / (LAYERS + 1), x_s[:, :, :], ALU.mult, ALU.add))
            seq(dve.tensor_scalar(dinv[:, 0, :], deg[:, :], 0.0, None, ALU.is_gt))
            dve.tensor_scalar(deg[:, :], deg[:, :], 1.0, None, ALU.max).then_inc(act_ask, 1)
            dve.wait_ge(act_done, 4)
            seq(dve.reciprocal(dinv[:, 1, :], dinv[:, 1, :]))
            seq(dve.tensor_tensor(out=dinv[:, 0, :], in0=dinv[:, 0, :], in1=dinv[:, 1, :], op=ALU.mult))
            seq(dve.tensor_scalar(dinv[:, 1, :], dinv[:, 0, :], 2.0, None, ALU.mult))
            for layer in range(LAYERS):
                seq(dve.tensor_tensor(out=work[:, :, :], in0=cur[:, :, :], in1=bc(dinv[:, 0, :], [Q, NB, D]), op=ALU.mult))
                for p in range(PARTS):
                    seq(dve.tensor_copy(parts[:, :, p, :], work[:, :, :]))
                    if p < PARTS - 1:
                        seq(dve.tensor_tensor(out=work[:, :, :], in0=work[:, :, :], in1=parts[:, :, p, :], op=ALU.subtract))
                dve.nop().then_inc(parts_ready, 1)
                for b in range(NB):
                    i = layer * NB + b
                    dve.wait_ge(prop_ready, i + 1)
                    pr = psum[i % 4][0:Q, 0:PARTS * D].rearrange("p (s f) -> p f s", s=PARTS)
                    dve.tensor_reduce(cur[:, b, :], pr, AX.X, ALU.add).then_inc(prop_taken, 1)
                dve.wait_ge(prop_taken, (layer + 1) * NB)
                seq(dve.tensor_tensor(out=cur[:, :, :], in0=cur[:, :, :], in1=bc(dinv[:, 1, :], [Q, NB, D]), op=ALU.mult))
                if layer < LAYERS - 1:
                    seq(dve.scalar_tensor_tensor(x_s[:, :, :], cur[:, :, :], 1.0 / (LAYERS + 1), x_s[:, :, :], ALU.mult, ALU.add))
            dve.scalar_tensor_tensor(work[:, :, :], cur[:, :, :], 1.0 / (LAYERS + 1), x_s[:, :, :], ALU.mult, ALU.add).then_inc(out_ready, 1)

        @block.tensor
        def _(pe):
            def project(bb):
                pe.wait_ge(tr_copied, 2 * bb + 2)
                c = bb // CH
                if bb % CH == 0 and c >= 2:
                    pe.wait_ge(proj_taken, c - 1)
                o = (bb % CH) * D
                for g in range(2):
                    last = pe.matmul(psum[2 + c % 2][0:Q, o:o + D], turned_s[:, (2 * bb + g) % 4, :], v_out[:, g, :],
                                     start=g == 0, stop=g == 1)
                last.then_inc(proj_ready, 1)

            for c in range(chunks):
                pe.wait_ge(mix_ready, c + 1)
                for b in range(CH):
                    for g in range(2):
                        i = (c * CH + b) * 2 + g
                        if i >= 2:
                            pe.wait_ge(tr_copied, i - 1)
                        pe.transpose(psum[i % 2][:, 0:Q], mix[:, c % 2, b, 2 * g:2 * g + 2, :].rearrange("p h f -> p (h f)"),
                                     ident[0:Q, 0:Q]).then_inc(tr_ready, 1)
                    if b > 0:
                        project(c * CH + b - 1)
                project(c * CH + CH - 1)
            by_block = counts[0:Q, 0:N * NB].rearrange("p (d s) -> p s d", s=NB)
            for layer in range(LAYERS):
                pe.wait_ge(parts_ready, layer + 1)
                for b in range(NB):
                    i = layer * NB + b
                    if i >= 4:
                        pe.wait_ge(prop_taken, i - 3)
                    for s in range(NB):
                        last = pe.matmul(psum[i % 4][0:Q, 0:PARTS * D], by_block[:, s, b * Q:(b + 1) * Q],
                                         parts[:, s, :, :].rearrange("p a f -> p (a f)"), start=s == 0, stop=s == NB - 1)
                    last.then_inc(prop_ready, 1)


def kernel(**inputs):
    import numpy as _np
    import concourse.bacc as _bacc
    from concourse import mybir as _mybir
    from concourse.bass_utils import run_bass_kernel_spmd as _run

    a = {k: _np.asarray(val) for k, val in inputs.items()}
    pad = PAIRS * EP - E
    src = _np.concatenate([a["src"], _np.zeros(pad, a["src"].dtype)])
    dst = _np.concatenate([a["dst"], _np.full(pad, NPAD - 1, a["dst"].dtype)])
    attr = _np.concatenate([a["edge_attr_16"], _np.zeros((pad, K), a["edge_attr_16"].dtype)])
    arrays = {
        "x": a["x"],
        "src_cols": src.reshape(PAIRS * 2, P).T,
        "dst_cols": dst.reshape(PAIRS * 2, P).T,
        "dst_row": dst.reshape(1, PAIRS * EP),
        "last_row": dst.reshape(1, PAIRS, EP)[:, :, -1],
        "attr_rows": attr.reshape(PAIRS, 2, P, K).transpose(0, 2, 1, 3),
        "attr_t": attr.T,
        "w": a["L0_gnn_W"],
        "w_t": a["L0_gnn_W"].T,
        "w_edge": a["L0_gnn_W_edge"],
        "att_src": a["L0_gnn_att_src"],
        "att_dst": a["L0_gnn_att_dst"],
        "att_edge": a["L0_gnn_att_edge"],
        "bias_t": a["L0_gnn_bias"].reshape(H, D).T,
        "wp": a["L0_gnn_Wp"],
        "bp": a["L0_gnn_bp"],
        "gamma": a["L0_gnn_gamma"],
        "beta": a["L0_gnn_beta"],
    }
    arrays = {f"in_{k}": _np.ascontiguousarray(val) for k, val in arrays.items()}
    nc = _bacc.Bacc("TRN2", target_bir_lowering=False, num_devices=1)
    args = {k[3:]: nc.dram_tensor(k, val.shape, _mybir.dt.from_np(val.dtype), kind="ExternalInput").ap()
            for k, val in arrays.items()}
    out = nc.dram_tensor("out", (N, D), _mybir.dt.float32, kind="ExternalOutput").ap()
    gnn_kernel(nc, out=out, **args)
    r = _run(nc, [arrays], core_ids=[0])
    return r.results[0]["out"]
```

```python
from contextlib import ExitStack

import concourse.bass as bass
from concourse import mybir

ALU = mybir.AluOpType
ACT = mybir.ActivationFunctionType
AX = mybir.AxisListType
F32 = mybir.dt.float32
F16 = mybir.dt.float16
BF16 = mybir.dt.bfloat16
I32 = mybir.dt.int32
I16 = mybir.dt.int16

P = 128
N = 3125
D = 64
H = 4
K = 16
E = 100000
Q = 125
NB = N // Q
W = 20
WINDOWS = -(-N // W)
NPAD = WINDOWS * W
EP = 256
PAIRS = 396
STEPS = PAIRS + WINDOWS - 1
WH = W * H
KEYS = W * NB
RING = 12
BATCH = 4
BATCHES = RING // BATCH
ROW = D + 1 + H
PARTS = 3
SUMS = PARTS * H + 1
SLOTS = SUMS + 1
AGG = D + 1 + SUMS
REC = AGG + 1
GROUP = 8
C_KEY, C_DST, C_SRC, C_IDX, C_LOGIT = 0, 2, 4, 6, 8
C_PARTS = C_LOGIT + 2 * H
COLS = C_PARTS + SLOTS
BIG = 2.0 ** 100
CLAMP = -1e20
LRELU = 0.2
EPS = 1e-5
LAYERS = 3
assert STEPS % RING == 0 and PAIRS * EP >= E and KEYS <= 512 and 2 * PAIRS % GROUP == 0


class Chain:

    def __init__(self, eng, sem, per_turn=0):
        self.eng, self.sem, self.per_turn = eng, sem, per_turn
        self.n, self.turn, self.local = 0, None, 0

    def enter_loop(self):
        self.base, self.local = self.n, 0

    def leave_loop(self, turns):
        assert self.local == self.per_turn, self.local
        self.turn = None
        self.n = self.base + turns * self.per_turn

    def did(self, ins):
        ins.then_inc(self.sem, 1)
        if self.turn is None:
            self.n += 1
            return self.n
        self.local += 1
        return (self.turn - 1) * self.per_turn + (self.base + self.local)

    def wait(self, value):
        self.eng.wait_ge(self.sem, value)

    def seq(self, ins):
        self.wait(self.did(ins))


def valid(j):
    return not isinstance(j, int) or 0 <= j < STEPS


def since(eng, sem, j, back, per=1):
    s = j - back
    if isinstance(s, int) and s < 0:
        return
    eng.wait_ge(sem, (s + 1) * per)


def gnn_kernel(nc, x, src_cols, dst_cols, last_row, attr_t, w, w_t, w_edge, att_src,
               att_dst, att_edge, bias_t, wp, bp, gamma, beta, out):
    hx_dram = nc.dram_tensor("hx_dram", [N, ROW], F32, kind="Internal").ap()
    ad_dram = nc.dram_tensor("ad_dram", [NPAD, H], F32, kind="Internal").ap()
    col_dram = nc.dram_tensor("col_dram", [P, PAIRS, COLS], F32, kind="Internal").ap()
    rec_dram = nc.dram_tensor("rec_dram", [STEPS, WH, REC], F32, kind="Internal").ap()

    with ExitStack() as ctx:
        def sem(name):
            return ctx.enter_context(nc.semaphore(name))

        def sb(name, shape, dt, where=ctx):
            return where.enter_context(nc.sbuf_tensor(name, shape, dt))

        psum = [ctx.enter_context(nc.psum_tensor(f"bank{i}", [P, 512], F32)) for i in range(8)]

        counts = sb("counts", [P, NPAD * NB], F16)
        ident = sb("ident", [P, P], F32)
        v_out = sb("v_out", [P, 2, D], F32)
        c_out = sb("c_out", [Q, D], F32)
        rec_row = sb("rec_row", [Q, NB], I32)

        held = ctx.enter_context(ExitStack())
        plain_sb = sb

        def sb(name, shape, dt, where=held):
            return plain_sb(name, shape, dt, where)

        key_off = sb("key_off", [P, STEPS], F32)
        restart = sb("restart", [P, STEPS], F32)
        keep = sb("keep", [P, STEPS], F32)
        where_i = sb("where_i", [1, 2, STEPS], I16)
        ad4_win = sb("ad4_win", [WH, WINDOWS], F32)

        stage = ctx.enter_context(ExitStack())
        prologue(nc, ctx, stage, psum, sem, sb, locals())
        stage.close()
        stage = ctx.enter_context(ExitStack())
        steps(nc, stage, psum, sem, sb, locals())
        stage.close()
        held.close()
        stage = ctx.enter_context(ExitStack())
        finish(nc, stage, psum, sem, sb, locals())


def prologue(nc, ctx, stage, psum, sem, sb, v):
    ident, v_out, c_out, rec_row = v["ident"], v["v_out"], v["c_out"], v["rec_row"]
    key_off, restart, keep, where_i = v["key_off"], v["restart"], v["keep"], v["where_i"]
    ad4_win, counts = v["ad4_win"], v["counts"]

    room = [0]

    def tmp(shape, dt, parts=P):
        size = 1
        for s in shape:
            size *= s
        n16 = size * (2 if dt in (F32, I32) else 1)
        ap = counts[0:parts, room[0]:room[0] + n16]
        room[0] += -(-n16 // 16) * 16
        assert room[0] <= NPAD * NB
        ap = ap.bitcast(dt) if dt != F16 else ap
        if len(shape) == 2:
            ap = ap.rearrange("p (a b) -> p a b", a=shape[0])
        elif len(shape) == 3:
            ap = ap.rearrange("p (a b c) -> p a b c", a=shape[0], b=shape[1])
        return ap

    def beside(name, shape, dt):
        return sb(name, shape, dt, stage)[:, :]

    xt = tmp([NB, D], F32, Q)
    sq = tmp([NB, D], F32, Q)
    hx = tmp([NB, ROW], F32, Q)
    a_d = tmp([NB, H], F32, Q)
    h_t = tmp([NB, Q], F32, D)
    stat = tmp([4, NB], F32, Q)
    w_sb = tmp([H * D], F32, D)
    w_ts = tmp([H, D], F32, D)
    wp_s = tmp([H, D], F32, D)
    bias_s = tmp([H], F32, D)
    att_s = tmp([H * D], F32, D)
    att_d = tmp([H * D], F32, D)
    fold = tmp([H * D], F32, D)
    a_sd = tmp([2 * H], F32, D)
    we_s = tmp([H * D], F32)
    att_e = tmp([H * D], F32)
    m_rep = tmp([H], F32)
    m_diag = tmp([GROUP, H], F32)
    tile_no = tmp([GROUP], F32)
    attr = tmp([2 * PAIRS // GROUP, P], F32)
    cols = tmp([PAIRS, COLS], F32)
    node = tmp([NB], F32, Q)
    node_w = tmp([NB], F32, Q)
    node_q = tmp([NB], F32, Q)
    node_i = tmp([NB], I32, Q)
    node_a = tmp([NB], F32, Q)
    node_c = tmp([NB], F32, Q)
    bp_b = tmp([D], F32, Q)
    last_b = tmp([PAIRS], I32)
    junk = tmp([PAIRS], F32)
    cnt = tmp([2], F32)
    start = tmp([2], F32)
    first = tmp([2], F32)
    edge_at = tmp([2], F32)
    began = tmp([2, STEPS], BF16)
    ones = tmp([P], BF16)
    step_no = tmp([STEPS], F32)
    win = tmp([STEPS], F32)
    same = tmp([STEPS], F32)
    t1 = tmp([STEPS], F32)
    row_i = tmp([2], I32)
    row_j = tmp([2], F32)
    src_i = beside("src_i", [P, 2 * PAIRS], I32)
    dst_i = beside("dst_i", [P, 2 * PAIRS], I32)
    s_f = beside("s_f", [P, 2 * PAIRS], F32)
    q_i = beside("q_i", [P, 2 * PAIRS], I32)
    q_f = beside("q_f", [P, 2 * PAIRS], F32)
    adj = beside("adj", [P, 2 * PAIRS], F32)
    rest = beside("rest", [P, 2 * PAIRS], F32)
    zero_h = tmp([H], F32)
    left_s = beside("left_s", [P, PAIRS * H], F32).rearrange("p (t h) -> p t h", h=H)
    logits = cols[:, :, C_LOGIT:C_LOGIT + 2 * H]
    parts = cols[:, :, C_PARTS:COLS]

    attr_in, col_ready, ael_ready, ael_copied, ad_back = (
        sem("attr_in"), sem("col_ready"), sem("ael_ready"), sem("ael_copied"), sem("ad_back"))
    x_in, w_in, e_in, l_in = sem("x_in"), sem("w_in"), sem("e_in"), sem("l_in")
    consts, dchain, gchain = sem("consts"), sem("pro_dve"), sem("pro_pool")
    var_ready, std_ready, h_ready, ht_ready, ht_copied = (
        sem("var_ready"), sem("std_ready"), sem("h_ready"), sem("ht_ready"), sem("ht_copied"))
    sd_ready, a_ready, hx_ready, m_ready, v_ready, v_copied = (
        sem("sd_ready"), sem("pro_a_ready"), sem("hx_ready"), sem("m_ready"), sem("v_ready"), sem("v_copied"))
    began_ready, win_ready, tables_out = sem("began_ready"), sem("win_ready"), sem("tables_out")

    W_LOADS = 8 + GROUP
    AE_ALL = 2 * PAIRS // GROUP
    AE_PER = 512 // (GROUP * H)
    AE_BANKS = -(-AE_ALL // AE_PER)
    with nc.Block() as block:
        @block.sync
        def _(sp):
            sp.dma_start(xt, v["x"].rearrange("(b p) f -> p b f", p=Q)).then_inc(x_in, 16)
            sp.dma_start(w_sb, v["w"][:, :]).then_inc(w_in, 16)
            sp.dma_start(att_s, v["att_src"].rearrange("h c -> (h c)")[None, :].to_broadcast([D, H * D])).then_inc(w_in, 16)
            sp.dma_start(att_d, v["att_dst"].rearrange("h c -> (h c)")[None, :].to_broadcast([D, H * D])).then_inc(w_in, 16)
            for g in range(GROUP):
                sp.dma_start(we_s[g * K:(g + 1) * K, :], v["w_edge"][:, :]).then_inc(w_in, 16)
            sp.dma_start(att_e, v["att_edge"].rearrange("h c -> (h c)")[None, :].to_broadcast([P, H * D])).then_inc(w_in, 16)
            sp.dma_start(w_ts, v["w_t"].rearrange("(h c) f -> c h f", h=H)).then_inc(w_in, 16)
            sp.dma_start(wp_s, v["wp"].rearrange("(h c) f -> c h f", h=H)).then_inc(w_in, 16)
            sp.dma_start(bias_s, v["bias_t"][:, :]).then_inc(w_in, 16)
            sp.dma_start(bp_b, v["bp"][None, :].to_broadcast([Q, D])).then_inc(w_in, 16)
            sp.dma_start(last_b, v["last_row"][:, :].to_broadcast([P, PAIRS])).then_inc(l_in, 16)
            sp.dma_start(attr, v["attr_t"][:, :, :]).then_inc(attr_in, 16)
            sp.dma_start(src_i, v["src_cols"][:, :]).then_inc(e_in, 16)
            sp.dma_start(dst_i, v["dst_cols"][:, :]).then_inc(e_in, 16)
            sp.wait_ge(hx_ready, 1)
            sp.dma_start(v["hx_dram"].rearrange("(b p) f -> p b f", p=Q), hx).then_inc(tables_out, 16)
            sp.dma_start(v["ad_dram"][0:N, :].rearrange("(b p) h -> p b h", p=Q), a_d).then_inc(tables_out, 16)
            sp.wait_ge(consts, 1)
            sp.dma_start(v["ad_dram"][N:NPAD, :], zero_h[0:NPAD - N, :]).then_inc(tables_out, 16)
            sp.wait_ge(tables_out, 3 * 16)
            sp.dma_start(ad4_win[:, :], v["ad_dram"].rearrange("(b w) h -> (w h) b", w=W),
                         allow_slow_non_contiguous=True).then_inc(ad_back, 16)
            sp.wait_ge(col_ready, 1)
            sp.dma_start(v["col_dram"][:, :, :], cols).then_inc(tables_out, 16)
            sp.wait_ge(tables_out, 4 * 16)

        @block.gpsimd
        def _(pool):
            chain = Chain(pool, gchain)
            pool.memset(zero_h, 0.0)
            pool.memset(ones, 1.0)
            pool.memset(hx[:, :, D:D + 1], 1.0)
            chain.seq(pool.memset(ident[:, :], 0.0))
            chain.seq(pool.affine_select(out=ident[:, :], in_=ident[:, :], compare_op=ALU.not_equal, fill=1.0, base=0,
                                         pattern=[[-1, P]], channel_multiplier=1))
            pool.iota(edge_at, pattern=[[P, 2]], base=1, channel_multiplier=1, allow_small_or_imprecise_dtypes=True)
            pool.iota(first, pattern=[[P * W, 2]], base=W, channel_multiplier=W, allow_small_or_imprecise_dtypes=True)
            pool.iota(row_i, pattern=[[0, 2]], base=0, channel_multiplier=1)
            pool.iota(tile_no, pattern=[[1, GROUP]], base=0, channel_multiplier=0, allow_small_or_imprecise_dtypes=True)
            pool.iota(node, pattern=[[Q, NB]], base=0, channel_multiplier=1, allow_small_or_imprecise_dtypes=True)
            pool.iota(step_no, pattern=[[1, STEPS]], base=0, channel_multiplier=0,
                      allow_small_or_imprecise_dtypes=True).then_inc(consts, 1)

        @block.scalar
        def _(act):
            act.wait_ge(var_ready, 1)
            act.activation(stat[:, 2, :], stat[:, 1, :], ACT.Sqrt).then_inc(std_ready, 1)
            for b in range(NB):
                act.wait_ge(ht_ready, b + 1)
                act.copy(h_t[:, b, :], psum[b % 2][0:D, 0:Q]).then_inc(ht_copied, 1)
            for i in range(AE_BANKS):
                act.wait_ge(ael_ready, i + 1)
                n0 = i * AE_PER
                n = min(AE_PER, AE_ALL - n0)
                act.copy(logits[:, n0 * GROUP // 2:(n0 + n) * GROUP // 2, :],
                         psum[i % 2][:, 0:n * GROUP * H].rearrange("p (t g) -> p t g", g=2 * H)).then_inc(ael_copied, 1)
            act.wait_ge(v_ready, 1)
            act.copy(v_out[:, :, :], psum[4][:, 0:2 * D].rearrange("p (g f) -> p g f", g=2)).then_inc(v_copied, 1)

        @block.vector
        def _(dve):
            chain = Chain(dve, dchain)
            seq = chain.seq
            dve.wait_ge(l_in, 16)
            dve.wait_ge(consts, 1)
            for g in range(2):
                seq(dve.tensor_scalar(junk, last_b, first[:, g:g + 1], 0.0, ALU.is_lt, ALU.add,
                                      accum_out=cnt[:, g:g + 1]))
            seq(dve.tensor_tensor(out=start, in0=cnt, in1=edge_at, op=ALU.add))
            for g in range(2):
                dve.tensor_scalar(began[:, g, :], step_no, start[:, g:g + 1], None, ALU.is_ge).then_inc(began_ready, 1)
            dve.wait_ge(w_in, W_LOADS * 16)
            for g, a in enumerate((att_s, att_d)):
                seq(dve.tensor_tensor(out=fold, in0=w_sb, in1=a, op=ALU.mult))
                seq(dve.tensor_reduce(a_sd[:, g * H:(g + 1) * H], fold.rearrange("p (h c) -> p h c", h=H), AX.X, ALU.add))
            seq(dve.tensor_tensor(out=we_s, in0=we_s, in1=att_e, op=ALU.mult))
            seq(dve.tensor_reduce(m_rep, we_s.rearrange("p (h c) -> p h c", h=H), AX.X, ALU.add))
            seq(dve.tensor_scalar(row_i, row_i, 4, None, ALU.arith_shift_right))
            seq(dve.tensor_copy(row_j, row_i))
            seq(dve.tensor_scalar(tile_no, tile_no, row_j[:, 0:1], None, ALU.is_equal))
            dve.tensor_tensor(out=m_diag, in0=m_rep[:, None, :].to_broadcast([P, GROUP, H]),
                              in1=tile_no.unsqueeze(2).to_broadcast([P, GROUP, H]), op=ALU.mult).then_inc(m_ready, 1)
            dve.wait_ge(x_in, 16)
            seq(dve.tensor_reduce(stat[:, 0, :], xt, AX.X, ALU.add))
            seq(dve.tensor_scalar(stat[:, 0, :], stat[:, 0, :], 1.0 / D, None, ALU.mult))
            seq(dve.tensor_tensor(out=xt, in0=xt, in1=stat[:, 0, :].unsqueeze(2).to_broadcast([Q, NB, D]), op=ALU.subtract))
            seq(dve.tensor_tensor(out=sq, in0=xt, in1=xt, op=ALU.mult))
            seq(dve.tensor_reduce(stat[:, 1, :], sq, AX.X, ALU.add))
            dve.tensor_scalar(stat[:, 1, :], stat[:, 1, :], 1.0 / D, EPS, ALU.mult, ALU.add).then_inc(var_ready, 1)
            dve.wait_ge(std_ready, 1)
            seq(dve.reciprocal(stat[:, 3, :], stat[:, 2, :]))
            seq(dve.tensor_tensor(out=xt, in0=xt, in1=stat[:, 3, :].unsqueeze(2).to_broadcast([Q, NB, D]), op=ALU.mult))
            dve.tensor_scalar(hx[:, :, 0:D], xt, 0.0, None, ALU.max).then_inc(h_ready, 1)
            def divide(rest, quot, quot_i, whole, by, adj):
                seq(dve.tensor_scalar(quot_i, whole, 1.0 / by, None, ALU.mult))
                seq(dve.tensor_copy(quot, quot_i))
                seq(dve.scalar_tensor_tensor(rest, quot, -float(by), whole, ALU.mult, ALU.add))
                for bound, op, sign in ((0.0, ALU.is_lt, 1.0), (float(by), ALU.is_ge, -1.0)):
                    seq(dve.tensor_scalar(adj, rest, bound, sign, op, ALU.mult))
                    seq(dve.scalar_tensor_tensor(rest, adj, float(by), rest, ALU.mult, ALU.add))
                    seq(dve.tensor_tensor(out=quot, in0=quot, in1=adj, op=ALU.subtract))

            def two(ap):
                return ap.rearrange("p (t a) -> p t a", a=2)

            dve.wait_ge(e_in, 32)
            seq(dve.tensor_copy(s_f, src_i))
            divide(rest, q_f, q_i, s_f, Q, adj)
            seq(dve.tensor_scalar(s_f, dst_i, float(NB), None, ALU.mult))
            seq(dve.tensor_tensor(out=cols[:, :, C_KEY:C_KEY + 2], in0=two(s_f), in1=two(q_f), op=ALU.add))
            seq(dve.tensor_copy(cols[:, :, C_DST:C_DST + 2], two(s_f)))
            seq(dve.tensor_copy(cols[:, :, C_SRC:C_SRC + 2], two(rest)))
            seq(dve.tensor_copy(cols[:, :, C_IDX:C_IDX + 2].bitcast(I32), two(src_i)))
            seq(dve.memset(parts, 0.0))
            dve.wait_ge(ael_copied, AE_BANKS)
            for a in range(2):
                half = parts[:, :, a * SLOTS // 2:(a + 1) * SLOTS // 2].bitcast(BF16)
                left = left_s
                seq(dve.tensor_copy(left, logits[:, :, a * H:(a + 1) * H]))
                for p in range(PARTS):
                    seq(dve.tensor_copy(half[:, :, p * H:(p + 1) * H], left))
                    if p < PARTS - 1:
                        seq(dve.tensor_tensor(out=left, in0=left, in1=half[:, :, p * H:(p + 1) * H], op=ALU.subtract))
                seq(dve.memset(half[:, :, SUMS - 1:SUMS], 1.0))
            dve.nop().then_inc(col_ready, 1)
            half = STEPS // 2
            dve.wait_ge(win_ready, 1)
            for g in range(2):
                seq(dve.tensor_copy(win[:, g * half:(g + 1) * half], psum[2 + g][:, 0:half]))
            seq(dve.tensor_scalar(key_off[:, :], win, -float(KEYS), None, ALU.mult))
            seq(dve.memset(keep[:, 0:1], 0.0))
            seq(dve.tensor_tensor(out=keep[:, 1:STEPS], in0=win[:, 1:STEPS], in1=win[:, 0:STEPS - 1], op=ALU.is_equal))
            seq(dve.tensor_scalar(restart[:, :], keep[:, :], 1.0, -BIG, ALU.subtract, ALU.mult))
            seq(dve.tensor_tensor(out=t1, in0=step_no, in1=win, op=ALU.subtract))
            seq(dve.tensor_copy(where_i[0:1, 0, :], t1[0:1, :]))
            seq(dve.tensor_copy(where_i[0:1, 1, :], win[0:1, :]))
            divide(node_w, node_q, node_i, node, W, node_a)
            seq(dve.tensor_scalar(node_a, node_q, 1.0, float(W), ALU.add, ALU.mult))
            for b in range(NB):
                seq(dve.tensor_scalar(junk[0:Q, :], last_b[0:Q, :], node_a[:, b:b + 1], 0.0, ALU.is_lt, ALU.add,
                                      accum_out=node_c[:, b:b + 1]))
            seq(dve.tensor_tensor(out=node_c, in0=node_c, in1=node_q, op=ALU.add))
            seq(dve.tensor_scalar(node_c, node_c, float(STEPS - 1), float(W), ALU.min, ALU.mult))
            seq(dve.tensor_tensor(out=rec_row[:, :], in0=node_c, in1=node_w, op=ALU.add))
            dve.wait_ge(a_ready, 1)
            pa = psum[5][0:Q, 0:NB * 2 * H].rearrange("p (b g) -> p b g", b=NB)
            seq(dve.tensor_copy(hx[:, :, D + 1:ROW], pa[:, :, 0:H]))
            dve.tensor_copy(a_d, pa[:, :, H:2 * H]).then_inc(hx_ready, 1)
            dve.wait_ge(v_ready, 2)
            seq(dve.tensor_tensor(out=c_out[:, :], in0=psum[6][0:Q, 0:D], in1=bp_b, op=ALU.add))
            dve.wait_ge(ad_back, 16)
            seq(dve.tensor_scalar(ad4_win[:, :], ad4_win[:, :], 4.0, None, ALU.mult))

        @block.tensor
        def _(pe):
            pe.wait_ge(consts, 1)
            pe.wait_ge(began_ready, 2)
            half = STEPS // 2
            for g in range(2):
                for s in range(2):
                    last = pe.matmul(psum[2 + g][:, 0:half], ones, began[:, s, g * half:(g + 1) * half],
                                     start=s == 0, stop=s == 1)
            last.then_inc(win_ready, 1)
            pe.wait_ge(w_in, W_LOADS * 16)
            for h in range(H):
                o = D * (h % 2)
                last = pe.matmul(psum[4][o:o + D, D * (h // 2):D * (h // 2) + D], w_ts[:, h, :], wp_s[:, h, :],
                                 start=True, stop=True)
            last.then_inc(v_ready, 1)
            for h in range(H):
                last = pe.matmul(psum[6][0:Q, 0:D], bias_s[:, h:h + 1].to_broadcast([D, Q]), wp_s[:, h, :],
                                 start=h == 0, stop=h == H - 1)
            last.then_inc(v_ready, 1)
            pe.wait_ge(h_ready, 1)
            for b in range(NB):
                if b >= 2:
                    pe.wait_ge(ht_copied, b - 1)
                pe.transpose(psum[b % 2][0:D, 0:Q], hx[:, b, 0:D], ident[0:Q, 0:Q]).then_inc(ht_ready, 1)
            pe.wait_ge(ht_copied, NB)
            for b in range(NB):
                last = pe.matmul(psum[5][0:Q, b * 2 * H:(b + 1) * 2 * H], h_t[:, b, :], a_sd, start=True, stop=True)
            last.then_inc(a_ready, 1)
            pe.wait_ge(m_ready, 1)
            pe.wait_ge(attr_in, 16)
            for i in range(AE_BANKS):
                if i >= 2:
                    pe.wait_ge(ael_copied, i - 1)
                n0 = i * AE_PER
                for g in range(n0, min(n0 + AE_PER, AE_ALL)):
                    o = (g - n0) * GROUP * H
                    last = pe.matmul(psum[i % 2][:, o:o + GROUP * H], attr[:, g, :],
                                     m_diag.rearrange("p t h -> p (t h)"), start=True, stop=True)
                last.then_inc(ael_ready, 1)


def steps(nc, stage, psum, sem, sb, v):
    ident, counts = v["ident"], v["counts"]
    key_off, restart, keep, where_i, ad4_win = v["key_off"], v["restart"], v["keep"], v["where_i"], v["ad4_win"]

    def t(name, shape, dt):
        return sb(name, shape, dt, stage)

    cols = t("cols", [P, RING, COLS], F32)
    rows = t("rows", [P, RING, 2, ROW], F32)
    u_wh = t("u_wh", [P, 2, 2, WH], F32)
    rel = t("rel", [P, RING, 4], F32)
    hot_key = t("hot_key", [P, 2, 2, KEYS], F16)
    hot_src = t("hot_src", [P, 2, 2, Q], F16)
    hot_dst = t("hot_dst", [P, RING, 2, WH], BF16)
    added = t("added", [Q, 2, KEYS], F16)
    relu4 = t("relu4", [WH, 2, EP], F32)
    logit = t("logit", [WH, 2, EP], F32)
    prob = t("prob", [WH, 2, EP], F32)
    weight = t("weight", [P, 2, 2, WH], F32)
    rec = t("rec", [WH, RING, REC], F32)
    top = t("top", [WH, RING], F32)
    before = t("before", [WH, RING], F32)
    m_neg = t("m_neg", [WH, RING], F32)
    scale = t("scale", [WH, RING], F32)
    num_key = t("num_key", [P, KEYS], F16)
    num_src = t("num_src", [P, Q], F16)
    num_dst = t("num_dst", [P, WH], F32)
    big_ident = t("big_ident", [P, P], BF16)
    one_row = t("one_row", [1, WH], BF16)
    big_row = t("big_row", [1, EP], BF16)

    consts, dchain = sem("step_consts"), sem("step_dve")
    zeroed, big_ready = sem("zeroed"), sem("big_ready")
    loaded = [sem(f"loaded{k}") for k in range(RING)]
    gathered = [sem(f"gathered{k}") for k in range(RING)]
    stored = [sem(f"stored{b}") for b in range(BATCHES)]
    rel_ready, hot_ready, spread = sem("rel_ready"), sem("hot_ready"), sem("spread")
    u_ready, relu_ready, logit_ready, prob_ready = sem("u_ready"), sem("relu_ready"), sem("logit_ready"), sem("prob_ready")
    turned, weight_ready, agg_ready, rec_ready = sem("turned"), sem("weight_ready"), sem("agg_ready"), sem("rec_ready")
    adj_ready, adj_copied, adj_added = sem("adj_ready"), sem("adj_copied"), sem("adj_added")

    ps_u = [psum[0], psum[1]]
    ps_w = [psum[2], psum[3]]
    ps_g = [psum[4], psum[5]]
    ps_a = [psum[6], psum[7]]
    CONSTS = 8
    CUTS = [0, WINDOWS // 4, WINDOWS // 2, WINDOWS]

    def slot_count(k, d, n, per):
        s = k + d
        return (s // RING + 1) * per if n is None else (n + (s // RING + 1)) * per

    def walk(eng, body, chain=None, looped=True):
        turns = STEPS // RING
        if not looped:
            for j in range(-RING, STEPS + RING):
                body(j, j, None)
            return
        for j in range(-RING, RING):
            body(j, j, None)
        with eng.Fori(1, turns - 1) as n:
            for k in range(RING):
                body(n * RING + k, k, n)
        for j in range((turns - 1) * RING, STEPS + RING):
            body(j, j, None)

    def load_row(eng, row, j, bound):
        _, vals = nc.values_load_multi_w_load_instructions(
            where_i[0:1, row, bass.ds(j, RING)], engines=(eng.engine,), min_val=0, max_val=bound,
            skip_runtime_bounds_check_because="the table is made within bounds")
        return vals

    with nc.Block() as block:
        @block.sync
        def _(sp):
            held = [None]

            def body(j, k, n):
                s = j - 1 - 4
                if (k - 5) % BATCH == BATCH - 1 and valid(s):
                    b = (k - 5) // BATCH % BATCHES
                    first = s - (BATCH - 1)
                    sp.wait_ge(rec_ready, s + 1)
                    sp.dma_start(v["rec_dram"][bass.ds(first, BATCH), :, :].rearrange("s q f -> q s f"),
                                 rec[:, b * BATCH:(b + 1) * BATCH, :]).then_inc(stored[b], 16)
                s = j + RING
                if valid(s):
                    if k % RING == 0:
                        held[0] = load_row(sp, 0, s, PAIRS - 1)
                    c = k % RING
                    since(sp, agg_ready, s, RING)
                    sp.dma_start(cols[:, c, :], v["col_dram"][:, bass.ds(held[0][c], 1), :].rearrange("p o f -> p (o f)")
                                 ).then_inc(loaded[c], 16)
            walk(sp, body)
            for b in range(BATCHES):
                sp.wait_ge(stored[b], STEPS // RING * 16)

        @block.gpsimd
        def _(pool):
            chain = Chain(pool, consts)
            free = dict(allow_small_or_imprecise_dtypes=True)
            chain.seq(pool.iota(num_key[:, :], pattern=[[1, KEYS]], base=0, channel_multiplier=0, **free))
            chain.seq(pool.iota(num_src[:, :], pattern=[[1, Q]], base=0, channel_multiplier=0, **free))
            chain.seq(pool.iota(num_dst[:, :], pattern=[[NB, W], [0, H]], base=0, channel_multiplier=0, **free))
            chain.seq(pool.memset(big_ident[:, :], 0.0))
            chain.seq(pool.affine_select(out=big_ident[:, :], in_=big_ident[:, :], compare_op=ALU.not_equal, fill=BIG,
                                         base=0, pattern=[[-1, P]], channel_multiplier=1))
            chain.seq(pool.memset(one_row[:, :], 1.0))
            chain.seq(pool.memset(big_row[:, :], -BIG))
            chain.seq(pool.memset(counts[:, 0:CUTS[1] * KEYS].bitcast(F32), 0.0))

            def body(j, k, n):
                s = j + 2
                if valid(s):
                    c = (k + 2) % RING
                    pool.wait_ge(gathered[c], slot_count(k, 2, n, 32))
                    since(pool, u_ready, s, 2)
                s2 = j + 6
                if valid(s2):
                    c2 = (k + 6) % RING
                    pool.wait_ge(loaded[c2], slot_count(k, 6, n, 16))
                    since(pool, agg_ready, s2, RING)
                if valid(s):
                    pool.tensor_tensor(out=u_wh[:, c % 2, :, :].rearrange("p a (w h) -> p a w h", w=W),
                                       in0=rows[:, c, :, None, D + 1:ROW].to_broadcast([P, 2, W, H]),
                                       in1=cols[:, c, C_LOGIT:C_PARTS].rearrange("p (a o h) -> p a o h", a=2, o=1).to_broadcast([P, 2, W, H]),
                                       op=ALU.add).then_inc(spread, 1)
                if valid(s2):
                    for a in range(2):
                        pool.indirect_dma_start(rows[:, c2, a, :], None, v["hx_dram"][:, :],
                                                bass.IndirectOffsetOnAxis(ap=cols[:, c2, C_IDX + a:C_IDX + a + 1].bitcast(I32), axis=0)
                                                ).then_inc(gathered[c2], 16)
            walk(pool, body)

        @block.scalar
        def _(act):
            held = [None]
            act.memzero(counts[:, CUTS[1] * KEYS:CUTS[2] * KEYS].bitcast(F32)).then_inc(zeroed, 1)

            def body(j, k, n):
                if k % RING == 0 and valid(j):
                    held[0] = load_row(act, 1, j, WINDOWS - 1)
                s = j + 2
                if valid(s):
                    c = (k + 2) % RING
                    act.wait_ge(loaded[c], slot_count(k, 2, n, 16))
                    since(act, hot_ready, s, RING)
                    act.activation(rel[:, c, :], cols[:, c, C_KEY:C_KEY + 4], ACT.Identity,
                                   bias=key_off[:, bass.ds(s, 1)]).then_inc(rel_ready, 1)
                s = j
                if valid(s):
                    c = k % RING
                    act.wait_ge(u_ready, s + 1)
                    since(act, logit_ready, s, 2)
                    act.activation(relu4[:, c % 2, :], ps_u[c % 2][0:WH, 0:EP], ACT.Relu, scale=4.0,
                                   bias=ad4_win[:, bass.ds(held[0][c], 1)]).then_inc(relu_ready, 1)
                s = j - 1
                if valid(s):
                    c = (k - 1) % RING
                    act.wait_ge(logit_ready, s + 1)
                    since(act, turned, s, 2)
                    since(act, rec_ready, s, RING)
                    act.activation(scale[:, c:c + 1], before[:, c:c + 1], ACT.Exp, scale=-1.0, bias=m_neg[:, c:c + 1])
                    act.activation(prob[:, c % 2, :], logit[:, c % 2, :], ACT.Exp, bias=m_neg[:, c:c + 1]).then_inc(prob_ready, 1)
                s = j
                if valid(s):
                    c = k % RING
                    act.wait_ge(adj_ready, s + 1)
                    since(act, adj_added, s, 2)
                    act.copy(added[:, c % 2, :], ps_a[c % 2][0:Q, 0:KEYS]).then_inc(adj_copied, 1)
                s = j - 2
                if valid(s):
                    c = (k - 2) % RING
                    act.wait_ge(turned, s + 1)
                    since(act, agg_ready, s, 2)
                    act.copy(weight[:, c % 2, :, :], ps_w[c % 2][:, 0:2 * WH].rearrange("p (a q) -> p a q", a=2)).then_inc(weight_ready, 1)
            walk(act, body)

        @block.vector
        def _(dve):
            held = [None]
            chain = Chain(dve, dchain)
            did = chain.did
            did(dve.memset(counts[:, CUTS[2] * KEYS:].bitcast(F32), 0.0))
            did(dve.memset(rec[:, :, :], 0.0))
            chain.seq(dve.memset(m_neg[:, :], 0.0))
            dve.wait_ge(consts, CONSTS)
            dve.wait_ge(zeroed, 1)

            def body(j, k, n):
                if k % RING == 0 and valid(j):
                    held[0] = load_row(dve, 1, j, WINDOWS - 1)
                s = j + 1
                if valid(s):
                    c = (k + 1) % RING
                    g = c % 2
                    dve.wait_ge(rel_ready, s + 1)
                    since(dve, adj_ready, s, 2)
                    since(dve, agg_ready, s, RING)
                    did(dve.tensor_tensor(out=hot_dst[:, c, :, :], in0=num_dst[:, None, :].to_broadcast([P, 2, WH]),
                                          in1=rel[:, c, 2:4].unsqueeze(2).to_broadcast([P, 2, WH]), op=ALU.is_equal))
                    for a in range(2):
                        did(dve.tensor_scalar(hot_src[:, g, a, :], num_src[:, :], cols[:, c, C_SRC + a:C_SRC + a + 1], 0.5,
                                              ALU.is_equal, ALU.mult))
                    did(dve.tensor_scalar(hot_key[:, g, 0, :], num_key[:, :], rel[:, c, 0:1], None, ALU.is_equal))
                    dve.tensor_scalar(hot_key[:, g, 1, :], num_key[:, :], rel[:, c, 1:2], None, ALU.is_equal).then_inc(hot_ready, 1)
                s = j
                if valid(s):
                    c = k % RING
                    prev = (c - 1) % RING
                    dve.wait_ge(relu_ready, s + 1)
                    since(dve, prob_ready, s, 2)
                    since(dve, logit_ready, s, 1)
                    did(dve.tensor_tensor(out=before[:, c:c + 1], in0=m_neg[:, prev:prev + 1], in1=restart[0:WH, bass.ds(s, 1)], op=ALU.add))
                    done = did(dve.tensor_tensor_reduce(out=logit[:, c % 2, :], in0=ps_u[c % 2][0:WH, 0:EP], in1=relu4[:, c % 2, :],
                                                        scale=LRELU, scalar=CLAMP, op0=ALU.add, op1=ALU.max,
                                                        accum_out=top[:, c:c + 1]))
                s = j - 1
                if valid(s):
                    b = last_b[0]
                    here = counts[0:Q, bass.ds(b * KEYS, KEYS)]
                    dve.wait_ge(adj_copied, s + 1)
                    since(dve, adj_added, s, 1)
                    dve.tensor_tensor(out=here, in0=added[:, (k - 1) % 2, :], in1=here, op=ALU.add).then_inc(adj_added, 1)
                s = j
                if valid(s):
                    last_b[0] = held[0][c]
                    chain.wait(done)
                    dve.scalar_tensor_tensor(m_neg[:, c:c + 1], top[:, c:c + 1], -1.0, before[:, c:c + 1], ALU.mult, ALU.min
                                             ).then_inc(logit_ready, 1)
                s = j - 4
                if valid(s):
                    c = (k - 4) % RING
                    prev = (c - 1) % RING
                    dve.wait_ge(agg_ready, s + 1)
                    if s % BATCH == 0 and s >= RING:
                        dve.wait_ge(stored[s // BATCH % BATCHES], s // RING * 16)
                    since(dve, rec_ready, s, 1)
                    dve.scalar_tensor_tensor(rec[:, c, 0:D + 1], rec[:, prev, 0:D + 1], scale[:, c:c + 1],
                                             ps_g[c % 2][0:WH, 0:D + 1], ALU.mult, ALU.add)
                    dve.tensor_copy(rec[:, c, AGG:REC], m_neg[:, c:c + 1])
                    dve.scalar_tensor_tensor(rec[:, c, D + 1:AGG], rec[:, prev, D + 1:AGG], keep[0:WH, bass.ds(s, 1)],
                                             ps_g[c % 2][0:WH, D + 1:AGG], ALU.mult, ALU.add).then_inc(rec_ready, 1)
            last_b = [None]
            walk(dve, body, looped=False)

        @block.tensor
        def _(pe):
            pe.wait_ge(consts, CONSTS)

            def body(j, k, n):
                s = j
                if valid(s):
                    c = k % RING
                    u = ps_u[c % 2][0:WH, 0:EP]
                    pe.wait_ge(hot_ready, s + 1)
                    since(pe, logit_ready, s, 2)
                    pe.matmul(u, one_row[:, :], big_row[:, :], start=True, stop=False)
                    for a in range(2):
                        pe.matmul(u[:, a * P:(a + 1) * P], hot_dst[:, c, a, :], big_ident[:, :], start=False, stop=False)
                    pe.wait_ge(spread, s + 1)
                    for a in range(2):
                        last = pe.matmul(u[:, a * P:(a + 1) * P], u_wh[:, c % 2, a, :], ident[:, :], start=False, stop=a == 1)
                    last.then_inc(u_ready, 1)
                    since(pe, adj_copied, s, 2)
                    for a in range(2):
                        last = pe.matmul(ps_a[c % 2][0:Q, 0:KEYS], hot_src[:, c % 2, a, :], hot_key[:, c % 2, a, :],
                                         start=a == 0, stop=a == 1)
                    last.then_inc(adj_ready, 1)
                s = j - 2
                if valid(s):
                    c = (k - 2) % RING
                    pe.wait_ge(prob_ready, s + 1)
                    since(pe, weight_ready, s, 2)
                    for a in range(2):
                        last = pe.transpose(ps_w[c % 2][:, a * WH:(a + 1) * WH], prob[:, c % 2, a * P:(a + 1) * P],
                                            ident[0:WH, 0:WH])
                    last.then_inc(turned, 1)
                s = j - 3
                if valid(s):
                    c = (k - 3) % RING
                    pe.wait_ge(weight_ready, s + 1)
                    since(pe, rec_ready, s, 2)
                    for a in range(2):
                        pe.matmul(ps_g[c % 2][0:WH, 0:D + 1], weight[:, c % 2, a, :], rows[:, c, a, 0:D + 1],
                                  start=a == 0, stop=a == 1)
                    for a in range(2):
                        edge = cols[:, c, C_PARTS + a * SLOTS // 2:C_PARTS + (a + 1) * SLOTS // 2].bitcast(BF16)
                        last = pe.matmul(ps_g[c % 2][0:WH, D + 1:AGG], hot_dst[:, c, a, :], edge[:, 0:SUMS],
                                         start=a == 0, stop=a == 1)
                    last.then_inc(agg_ready, 1)
            walk(pe, body)


def finish(nc, stage, psum, sem, sb, v):
    ident, counts, v_out, c_out = v["ident"], v["counts"], v["v_out"], v["c_out"]

    def t(name, shape, dt):
        return sb(name, shape, dt, stage)

    CH = 5
    agg = t("agg", [Q, 2, CH, H, REC], F32)
    hx = t("hx", [Q, NB, ROW], F32)
    a_d = t("a_d", [Q, NB, H], F32)
    x_s = t("x_s", [Q, NB, D], F32)
    g_b = t("g_b", [Q, 2, D], F32)
    small = t("small", [Q, 8, CH, H], F32)
    deg = t("deg", [Q, NB], F32)
    cmax = t("cmax", [Q, 2, CH], F32)
    mix = t("mix", [Q, 2, CH, H, D], F32)
    turned_s = t("turned_s", [P, 4, Q], F32)
    cur = t("cur", [Q, NB, D], F32)
    work = t("work", [Q, NB, D], F32)
    stat = t("stat", [Q, 4, NB], F32)
    dinv = t("dinv", [Q, 2, NB], F32)
    mix2 = work[:, :, :].rearrange("p b f -> p (b f)")[:, 0:CH * H * D].rearrange("p (b h f) -> p b h f", b=CH, h=H)
    parts = mix[:, :, :, :, :].rearrange("p a b h f -> p (a b h f)").bitcast(BF16)[:, 0:NB * PARTS * D].rearrange(
        "p (b s f) -> p b s f", b=NB, s=PARTS)

    in_s, rec_in = sem("fin_in"), [sem("rec_in0"), sem("rec_in1")]
    dchain = sem("fin_dve")
    diff, exps = sem("fin_diff"), sem("fin_exps")
    mix_ready, tr_ready, tr_copied, proj_ready, proj_taken = (
        sem("mix_ready"), sem("tr_ready"), sem("tr_copied"), sem("proj_ready"), sem("proj_taken"))
    act_ask, act_done = sem("act_ask"), sem("act_done")
    parts_ready, prop_ready, prop_taken = sem("parts_ready"), sem("prop_ready"), sem("prop_taken")
    out_ready, out_done = sem("out_ready"), sem("out_done")
    chunks = NB // CH

    def bc(ap, shape):
        return ap.unsqueeze(len(shape) - 1).to_broadcast(shape)

    with nc.Block() as block:
        @block.sync
        def _(sp):
            sp.dma_start(hx[:, :, :], v["hx_dram"].rearrange("(b p) f -> p b f", p=Q)).then_inc(in_s, 16)
            sp.dma_start(a_d[:, :, :], v["ad_dram"][0:N, :].rearrange("(b p) h -> p b h", p=Q)).then_inc(in_s, 16)
            sp.dma_start(x_s[:, :, :], v["x"].rearrange("(b p) f -> p b f", p=Q)).then_inc(in_s, 16)
            sp.dma_start(g_b[:, 0, :], v["gamma"][None, :].to_broadcast([Q, D])).then_inc(in_s, 16)
            sp.dma_start(g_b[:, 1, :], v["beta"][None, :].to_broadcast([Q, D])).then_inc(in_s, 16)
            sp.wait_ge(out_ready, 1)
            sp.dma_start(v["out"].rearrange("(b p) f -> p b f", p=Q), work[:, :, :]).then_inc(out_done, 16)
            sp.wait_ge(out_done, 16)

        @block.gpsimd
        def _(pool):
            nodes = v["rec_dram"].rearrange("s (w h) f -> (s w) (h f)", h=H)
            for c in range(chunks):
                if c >= 2:
                    pool.wait_ge(mix_ready, c - 1)
                for b in range(CH):
                    pool.indirect_dma_start(agg[:, c % 2, b, :, :].rearrange("p h f -> p (h f)"), None, nodes,
                                            bass.IndirectOffsetOnAxis(ap=v["rec_row"][:, c * CH + b:c * CH + b + 1], axis=0)
                                            ).then_inc(rec_in[c % 2], 16)

        @block.scalar
        def _(act):
            for c in range(chunks):
                act.wait_ge(diff, c + 1)
                act.activation(small[:, 4:6, :, :], small[:, 2:4, :, :], ACT.Exp).then_inc(exps, 1)
                for b in range(CH):
                    for g in range(2):
                        i = (c * CH + b) * 2 + g
                        act.wait_ge(tr_ready, i + 1)
                        if i >= 4:
                            act.wait_ge(proj_ready, (i - 4) // 2 + 1)
                        act.copy(turned_s[:, i % 4, :], psum[i % 2][:, 0:Q]).then_inc(tr_copied, 1)
            act.wait_ge(act_ask, 1)
            act.activation(work[:, :, :], work[:, :, :], ACT.Exp).then_inc(act_done, 1)
            for i in range(2):
                act.wait_ge(act_ask, i + 2)
                act.activation(stat[:, 2, :], stat[:, 1, :], ACT.Sqrt).then_inc(act_done, 1)
            act.wait_ge(act_ask, 4)
            act.activation(dinv[:, 1, :], deg[:, :], ACT.Sqrt).then_inc(act_done, 1)

        @block.vector
        def _(dve):
            chain = Chain(dve, dchain)
            seq = chain.seq
            dve.wait_ge(in_s, 5 * 16)
            for c in range(chunks):
                blocks = slice(c * CH, (c + 1) * CH)
                a = agg[:, c % 2, :, :, :]
                dve.wait_ge(rec_in[c % 2], (c // 2 + 1) * 16 * CH)
                cnt = a[:, :, 0, AGG - 1]
                seq(dve.tensor_copy(deg[:, blocks], cnt))
                seq(dve.tensor_scalar(cmax[:, 0, :], cnt, 1.0, None, ALU.max))
                seq(dve.reciprocal(cmax[:, 1, :], cmax[:, 0, :]))
                sums = a[:, :, 0, D + 1:D + 1 + PARTS * H].rearrange("p b (s h) -> p b h s", s=PARTS)
                seq(dve.tensor_reduce(small[:, 0, :, :], sums, AX.X, ALU.add))
                seq(dve.tensor_tensor(out=small[:, 0, :, :], in0=small[:, 0, :, :], in1=bc(cmax[:, 1, :], [Q, CH, H]), op=ALU.mult))
                seq(dve.tensor_tensor(out=small[:, 0, :, :], in0=small[:, 0, :, :], in1=hx[:, blocks, D + 1:ROW], op=ALU.add))
                seq(dve.tensor_tensor(out=small[:, 0, :, :], in0=small[:, 0, :, :], in1=a_d[:, blocks, :], op=ALU.add))
                seq(dve.scalar_tensor_tensor(small[:, 1, :, :], small[:, 0, :, :], LRELU, small[:, 0, :, :], ALU.mult, ALU.max))
                seq(dve.scalar_tensor_tensor(small[:, 2, :, :], a_d[:, blocks, :], LRELU, a[:, :, :, AGG], ALU.mult, ALU.subtract))
                m_e = small[:, 2, :, :]
                seq(dve.tensor_tensor(out=small[:, 0, :, :], in0=small[:, 1, :, :], in1=m_e, op=ALU.max))
                seq(dve.tensor_tensor(out=small[:, 2, :, :], in0=m_e, in1=small[:, 0, :, :], op=ALU.subtract))
                dve.tensor_tensor(out=small[:, 3, :, :], in0=small[:, 1, :, :], in1=small[:, 0, :, :], op=ALU.subtract).then_inc(diff, 1)
                dve.wait_ge(exps, c + 1)
                seq(dve.tensor_tensor(out=small[:, 6, :, :], in0=small[:, 4, :, :], in1=a[:, :, :, D], op=ALU.mult))
                seq(dve.tensor_tensor(out=small[:, 6, :, :], in0=small[:, 6, :, :], in1=small[:, 5, :, :], op=ALU.add))
                seq(dve.reciprocal(small[:, 7, :, :], small[:, 6, :, :]))
                for g in (4, 5):
                    seq(dve.tensor_tensor(out=small[:, g, :, :], in0=small[:, g, :, :], in1=small[:, 7, :, :], op=ALU.mult))
                if c >= 2:
                    dve.wait_ge(tr_ready, (c - 1) * CH * 2)
                mx = mix[:, c % 2, :, :, :]
                for h in range(H):
                    did = chain.did(dve.tensor_tensor(out=mx[:, :, h, :], in0=a[:, :, h, 0:D], in1=bc(small[:, 4, :, h], [Q, CH, D]), op=ALU.mult))
                    did = chain.did(dve.tensor_tensor(out=mix2[:, :, h, :], in0=hx[:, blocks, 0:D], in1=bc(small[:, 5, :, h], [Q, CH, D]), op=ALU.mult))
                chain.wait(did)
                dve.tensor_tensor(out=mx, in0=mx, in1=mix2[:, :, :, :], op=ALU.add).then_inc(mix_ready, 1)
                dve.wait_ge(mix_ready, c + 1)
                dve.wait_ge(proj_ready, (c + 1) * CH)
                pr = psum[2 + c % 2][0:Q, 0:CH * D].rearrange("p (b f) -> p b f", b=CH)
                dve.tensor_tensor(out=cur[:, blocks, :], in0=pr, in1=c_out[:, None, :].to_broadcast([Q, CH, D]), op=ALU.add).then_inc(proj_taken, 1)
            dve.wait_ge(proj_taken, chunks)
            dve.tensor_scalar(work[:, :, :], cur[:, :, :], 0.0, None, ALU.min).then_inc(act_ask, 1)
            dve.wait_ge(act_done, 1)
            seq(dve.tensor_scalar(cur[:, :, :], cur[:, :, :], 0.0, None, ALU.max))
            seq(dve.scalar_tensor_tensor(cur[:, :, :], work[:, :, :], -1.0, cur[:, :, :], ALU.add, ALU.add))
            seq(dve.tensor_tensor(out=cur[:, :, :], in0=cur[:, :, :], in1=hx[:, :, 0:D], op=ALU.add))

            def norm(i):
                seq(dve.tensor_reduce(stat[:, 0, :], cur[:, :, :], AX.X, ALU.add))
                seq(dve.tensor_scalar(stat[:, 0, :], stat[:, 0, :], 1.0 / D, None, ALU.mult))
                seq(dve.tensor_tensor(out=cur[:, :, :], in0=cur[:, :, :], in1=bc(stat[:, 0, :], [Q, NB, D]), op=ALU.subtract))
                seq(dve.tensor_tensor(out=work[:, :, :], in0=cur[:, :, :], in1=cur[:, :, :], op=ALU.mult))
                seq(dve.tensor_reduce(stat[:, 1, :], work[:, :, :], AX.X, ALU.add))
                dve.tensor_scalar(stat[:, 1, :], stat[:, 1, :], 1.0 / D, EPS, ALU.mult, ALU.add).then_inc(act_ask, 1)
                dve.wait_ge(act_done, i + 2)
                seq(dve.reciprocal(stat[:, 3, :], stat[:, 2, :]))
                seq(dve.tensor_tensor(out=cur[:, :, :], in0=cur[:, :, :], in1=bc(stat[:, 3, :], [Q, NB, D]), op=ALU.mult))

            norm(0)
            seq(dve.tensor_tensor(out=cur[:, :, :], in0=cur[:, :, :], in1=g_b[:, 0, None, :].to_broadcast([Q, NB, D]), op=ALU.mult))
            seq(dve.tensor_tensor(out=cur[:, :, :], in0=cur[:, :, :], in1=g_b[:, 1, None, :].to_broadcast([Q, NB, D]), op=ALU.add))
            seq(dve.tensor_tensor(out=x_s[:, :, :], in0=x_s[:, :, :], in1=cur[:, :, :], op=ALU.add))
            seq(dve.tensor_copy(cur[:, :, :], x_s[:, :, :]))
            norm(1)
            seq(dve.tensor_scalar(cur[:, :, :], cur[:, :, :], 0.0, None, ALU.max))
            seq(dve.scalar_tensor_tensor(x_s[:, :, :], cur[:, :, :], 1.0 / (LAYERS + 1), x_s[:, :, :], ALU.mult, ALU.add))
            seq(dve.tensor_scalar(dinv[:, 0, :], deg[:, :], 0.0, None, ALU.is_gt))
            dve.tensor_scalar(deg[:, :], deg[:, :], 1.0, None, ALU.max).then_inc(act_ask, 1)
            dve.wait_ge(act_done, 4)
            seq(dve.reciprocal(dinv[:, 1, :], dinv[:, 1, :]))
            seq(dve.tensor_tensor(out=dinv[:, 0, :], in0=dinv[:, 0, :], in1=dinv[:, 1, :], op=ALU.mult))
            seq(dve.tensor_scalar(dinv[:, 1, :], dinv[:, 0, :], 2.0, None, ALU.mult))
            for layer in range(LAYERS):
                seq(dve.tensor_tensor(out=work[:, :, :], in0=cur[:, :, :], in1=bc(dinv[:, 0, :], [Q, NB, D]), op=ALU.mult))
                for p in range(PARTS):
                    seq(dve.tensor_copy(parts[:, :, p, :], work[:, :, :]))
                    if p < PARTS - 1:
                        seq(dve.tensor_tensor(out=work[:, :, :], in0=work[:, :, :], in1=parts[:, :, p, :], op=ALU.subtract))
                dve.nop().then_inc(parts_ready, 1)
                for b in range(NB):
                    i = layer * NB + b
                    dve.wait_ge(prop_ready, i + 1)
                    pr = psum[i % 4][0:Q, 0:PARTS * D].rearrange("p (s f) -> p f s", s=PARTS)
                    dve.tensor_reduce(cur[:, b, :], pr, AX.X, ALU.add).then_inc(prop_taken, 1)
                dve.wait_ge(prop_taken, (layer + 1) * NB)
                seq(dve.tensor_tensor(out=cur[:, :, :], in0=cur[:, :, :], in1=bc(dinv[:, 1, :], [Q, NB, D]), op=ALU.mult))
                if layer < LAYERS - 1:
                    seq(dve.scalar_tensor_tensor(x_s[:, :, :], cur[:, :, :], 1.0 / (LAYERS + 1), x_s[:, :, :], ALU.mult, ALU.add))
            dve.scalar_tensor_tensor(work[:, :, :], cur[:, :, :], 1.0 / (LAYERS + 1), x_s[:, :, :], ALU.mult, ALU.add).then_inc(out_ready, 1)

        @block.tensor
        def _(pe):
            def project(bb):
                pe.wait_ge(tr_copied, 2 * bb + 2)
                c = bb // CH
                if bb % CH == 0 and c >= 2:
                    pe.wait_ge(proj_taken, c - 1)
                o = (bb % CH) * D
                for g in range(2):
                    last = pe.matmul(psum[2 + c % 2][0:Q, o:o + D], turned_s[:, (2 * bb + g) % 4, :], v_out[:, g, :],
                                     start=g == 0, stop=g == 1)
                last.then_inc(proj_ready, 1)

            for c in range(chunks):
                pe.wait_ge(mix_ready, c + 1)
                for b in range(CH):
                    for g in range(2):
                        i = (c * CH + b) * 2 + g
                        if i >= 2:
                            pe.wait_ge(tr_copied, i - 1)
                        pe.transpose(psum[i % 2][:, 0:Q], mix[:, c % 2, b, 2 * g:2 * g + 2, :].rearrange("p h f -> p (h f)"),
                                     ident[0:Q, 0:Q]).then_inc(tr_ready, 1)
                    if b > 0:
                        project(c * CH + b - 1)
                project(c * CH + CH - 1)
            by_block = counts[0:Q, 0:N * NB].rearrange("p (d s) -> p s d", s=NB)
            for layer in range(LAYERS):
                pe.wait_ge(parts_ready, layer + 1)
                for b in range(NB):
                    i = layer * NB + b
                    if i >= 4:
                        pe.wait_ge(prop_taken, i - 3)
                    for s in range(NB):
                        last = pe.matmul(psum[i % 4][0:Q, 0:PARTS * D], by_block[:, s, b * Q:(b + 1) * Q],
                                         parts[:, s, :, :].rearrange("p a f -> p (a f)"), start=s == 0, stop=s == NB - 1)
                    last.then_inc(prop_ready, 1)


def kernel(**inputs):
    import numpy as _np
    import concourse.bacc as _bacc
    from concourse import mybir as _mybir
    from concourse.bass_utils import run_bass_kernel_spmd as _run

    a = {k: _np.asarray(val) for k, val in inputs.items()}
    pad = PAIRS * EP - E
    src = _np.concatenate([a["src"], _np.zeros(pad, a["src"].dtype)])
    dst = _np.concatenate([a["dst"], _np.full(pad, NPAD - 1, a["dst"].dtype)])
    attr = _np.concatenate([a["edge_attr_16"], _np.zeros((pad, K), a["edge_attr_16"].dtype)])
    arrays = {
        "x": a["x"],
        "src_cols": src.reshape(PAIRS * 2, P).T,
        "dst_cols": dst.reshape(PAIRS * 2, P).T,
        "last_row": dst.reshape(1, PAIRS, EP)[:, :, -1],
        "attr_t": attr.reshape(2 * PAIRS // GROUP, GROUP, P, K).transpose(1, 3, 0, 2).reshape(GROUP * K, -1, P),
        "w": a["L0_gnn_W"],
        "w_t": a["L0_gnn_W"].T,
        "w_edge": a["L0_gnn_W_edge"],
        "att_src": a["L0_gnn_att_src"],
        "att_dst": a["L0_gnn_att_dst"],
        "att_edge": a["L0_gnn_att_edge"],
        "bias_t": a["L0_gnn_bias"].reshape(H, D).T,
        "wp": a["L0_gnn_Wp"],
        "bp": a["L0_gnn_bp"],
        "gamma": a["L0_gnn_gamma"],
        "beta": a["L0_gnn_beta"],
    }
    arrays = {f"in_{k}": _np.ascontiguousarray(val) for k, val in arrays.items()}
    nc = _bacc.Bacc("TRN2", target_bir_lowering=False, num_devices=1)
    args = {k[3:]: nc.dram_tensor(k, val.shape, _mybir.dt.from_np(val.dtype), kind="ExternalInput").ap()
            for k, val in arrays.items()}
    out = nc.dram_tensor("out", (N, D), _mybir.dt.float32, kind="ExternalOutput").ap()
    gnn_kernel(nc, out=out, **args)
    r = _run(nc, [arrays], core_ids=[0])
    return r.results[0]["out"]
```
